# Optimizing a Trainium2 kernel written in Bass

```python
import numpy as np
import jax
import jax.numpy as jnp

def _softmax(x, axis=-1):
    return jax.nn.softmax(x, axis=axis)

def _gelu(x):
    return jax.nn.gelu(x, approximate=True)

def _silu(x):
    return jax.nn.silu(x)

def _sigmoid(x):
    return jax.nn.sigmoid(x)

def _layernorm(x, axis=-1, eps=1e-05):
    m = jnp.mean(x, axis=axis, keepdims=True)
    v = jnp.var(x, axis=axis, keepdims=True)
    return (x - m) / jnp.sqrt(v + eps)

def _scatter_add(tgt, idx, src, axis=0):
    return tgt.at[idx].add(src)

def _segment_sum(src, seg, n):
    return jax.ops.segment_sum(src, seg, n)
kernel_name = 'mk_recurrent_d1_jaxref_r8_4167d1'

def setup_inputs(seed: int=0):
    np.random.seed(seed)
    _w = jnp.asarray

    def _L0_attn_setup():
        import jax, jax.numpy as jnp
        import numpy as np
        L, H, D, DH, DF = (4, 16, 128, 64, 512)
        B, S = (4, 128)

        def layer_norm(x, g, b):
            mu = jnp.mean(x, axis=-1, keepdims=True)
            var = jnp.mean((x - mu) ** 2, axis=-1, keepdims=True)
            return (x - mu) * jax.lax.rsqrt(var + 1e-05) * g + b

        def pos_encoding(seq_len, d):
            pos = jnp.arange(seq_len - 1, -1, -1, dtype=jnp.float32)
            freq = 1.0 / 10000.0 ** (jnp.arange(0, d, 2, dtype=jnp.float32) / d)
            ang = pos[:, None] * freq[None, :]
            return jnp.concatenate([jnp.sin(ang), jnp.cos(ang)], axis=-1)
        key = jax.random.key(seed)
        ks = jax.random.split(key, 16)
        s = 0.02
        return {'x': jax.random.normal(ks[0], (B, S, D), jnp.float32), 'W_qkv': jax.random.normal(ks[1], (L, D, 3 * H * DH), jnp.float32) * s, 'W_r': jax.random.normal(ks[2], (L, D, H * DH), jnp.float32) * s, 'W_o': jax.random.normal(ks[3], (L, H * DH, D), jnp.float32) * s, 'u': jax.random.normal(ks[4], (H, DH), jnp.float32) * s, 'v': jax.random.normal(ks[5], (H, DH), jnp.float32) * s, 'ln1_g': jnp.ones((L, D), jnp.float32), 'ln1_b': jnp.zeros((L, D), jnp.float32), 'W_ff1': jax.random.normal(ks[6], (L, D, DF), jnp.float32) * s, 'b_ff1': jnp.zeros((L, DF), jnp.float32), 'W_ff2': jax.random.normal(ks[7], (L, DF, D), jnp.float32) * s, 'b_ff2': jnp.zeros((L, D), jnp.float32), 'ln2_g': jnp.ones((L, D), jnp.float32), 'ln2_b': jnp.zeros((L, D), jnp.float32)}
    _L0_attn_in = _L0_attn_setup()

    def _L0_ffn_setup():
        import jax, jax.numpy as jnp
        import numpy as np
        K = 2
        key = jax.random.key(seed)
        ks = jax.random.split(key, 6)
        B, S, D, U, E = (2, 256, 128, 512, 8)
        return {'x': jax.random.normal(ks[0], (B, S, D), dtype=jnp.float32), 'w_router': jax.random.normal(ks[1], (E, D), dtype=jnp.float32), 'w_up': jax.random.normal(ks[2], (E, U, D), dtype=jnp.float32), 'b_up': jax.random.normal(ks[3], (E, U), dtype=jnp.float32), 'w_down': jax.random.normal(ks[4], (E, D, U), dtype=jnp.float32), 'b_down': jax.random.normal(ks[5], (E, D), dtype=jnp.float32)}
    _L0_ffn_in = _L0_ffn_setup()
    _d = {'L0_attn_x': _L0_attn_in['x'], 'L0_attn_W_qkv': _L0_attn_in['W_qkv'], 'L0_attn_W_r': _L0_attn_in['W_r'], 'L0_attn_W_o': _L0_attn_in['W_o'], 'L0_attn_u': _L0_attn_in['u'], 'L0_attn_v': _L0_attn_in['v'], 'L0_attn_ln1_g': _L0_attn_in['ln1_g'], 'L0_attn_ln1_b': _L0_attn_in['ln1_b'], 'L0_attn_W_ff1': _L0_attn_in['W_ff1'], 'L0_attn_b_ff1': _L0_attn_in['b_ff1'], 'L0_attn_W_ff2': _L0_attn_in['W_ff2'], 'L0_attn_b_ff2': _L0_attn_in['b_ff2'], 'L0_attn_ln2_g': _L0_attn_in['ln2_g'], 'L0_attn_ln2_b': _L0_attn_in['ln2_b'], 'L0_ffn_w_router': _L0_ffn_in['w_router'], 'L0_ffn_w_up': _L0_ffn_in['w_up'], 'L0_ffn_b_up': _L0_ffn_in['b_up'], 'L0_ffn_w_down': _L0_ffn_in['w_down'], 'L0_ffn_b_down': _L0_ffn_in['b_down']}
    _x0 = _d['L0_attn_x']
    _d['L0_attn_x'] = jax.random.normal(jax.random.fold_in(jax.random.key(seed), 1), (2, 1024, 128), dtype=_x0.dtype)
    del _x0
    return _d

def reference(L0_attn_x, L0_attn_W_qkv, L0_attn_W_r, L0_attn_W_o, L0_attn_u, L0_attn_v, L0_attn_ln1_g, L0_attn_ln1_b, L0_attn_W_ff1, L0_attn_b_ff1, L0_attn_W_ff2, L0_attn_b_ff2, L0_attn_ln2_g, L0_attn_ln2_b, L0_ffn_w_router, L0_ffn_w_up, L0_ffn_b_up, L0_ffn_w_down, L0_ffn_b_down):

    def _L0_attn_ref(x, W_qkv, W_r, W_o, u, v, ln1_g, ln1_b, W_ff1, b_ff1, W_ff2, b_ff2, ln2_g, ln2_b):
        import jax, jax.numpy as jnp
        import numpy as np
        L, H, D, DH, DF = (4, 16, 128, 64, 512)
        B, S = (4, 128)

        def layer_norm(x, g, b):
            mu = jnp.mean(x, axis=-1, keepdims=True)
            var = jnp.mean((x - mu) ** 2, axis=-1, keepdims=True)
            return (x - mu) * jax.lax.rsqrt(var + 1e-05) * g + b

        def pos_encoding(seq_len, d):
            pos = jnp.arange(seq_len - 1, -1, -1, dtype=jnp.float32)
            freq = 1.0 / 10000.0 ** (jnp.arange(0, d, 2, dtype=jnp.float32) / d)
            ang = pos[:, None] * freq[None, :]
            return jnp.concatenate([jnp.sin(ang), jnp.cos(ang)], axis=-1)
        b, s_len, _ = x.shape
        r = pos_encoding(s_len, D)
        h = x
        inv_sqrt_d = 1.0 / jnp.sqrt(jnp.float32(DH))
        for i in range(L):
            qkv = h @ W_qkv[i]
            q, k, val = jnp.split(qkv, 3, axis=-1)
            q = q.reshape(b, s_len, H, DH)
            k = k.reshape(b, s_len, H, DH)
            val = val.reshape(b, s_len, H, DH)
            kr = (r @ W_r[i]).reshape(s_len, H, DH)
            AC = jnp.einsum('bqhd,bkhd->bhqk', q + u, k)
            BD = jnp.einsum('bqhd,khd->bhqk', q + v, kr)
            prob = jax.nn.softmax((AC + BD) * inv_sqrt_d, axis=-1)
            vec = jnp.einsum('bhqk,bkhd->bqhd', prob, val).reshape(b, s_len, H * DH)
            h = layer_norm(h + vec @ W_o[i], ln1_g[i], ln1_b[i])
            ff = jax.nn.relu(h @ W_ff1[i] + b_ff1[i]) @ W_ff2[i] + b_ff2[i]
            h = layer_norm(ff, ln2_g[i], ln2_b[i])
        return h

    def _L0_ffn_ref(x, w_router, w_up, b_up, w_down, b_down):
        import jax, jax.numpy as jnp
        import numpy as np
        K = 2
        logits = jnp.einsum('bsd,ed->bse', x, w_router)
        top_logits, idx = jax.lax.top_k(logits, K)
        router_weights = jax.nn.softmax(top_logits, axis=-1)
        h = jnp.einsum('eud,bsd->bseu', w_up, x) + b_up[None, None]
        h = jax.nn.gelu(h, approximate=False)
        y = jnp.einsum('edu,bseu->bsed', w_down, h) + b_down[None, None]
        y_k = jnp.take_along_axis(y, idx[..., None], axis=2)
        out = jnp.einsum('bskd,bsk->bsd', y_k, router_weights)
        return out
    x = L0_attn_x
    xn = _layernorm(x, axis=-1)
    s = _L0_attn_ref(xn, L0_attn_W_qkv, L0_attn_W_r, L0_attn_W_o, L0_attn_u, L0_attn_v, L0_attn_ln1_g, L0_attn_ln1_b, L0_attn_W_ff1, L0_attn_b_ff1, L0_attn_W_ff2, L0_attn_b_ff2, L0_attn_ln2_g, L0_attn_ln2_b)
    g = _silu(_L0_ffn_ref(xn, L0_ffn_w_router, L0_ffn_w_up, L0_ffn_b_up, L0_ffn_w_down, L0_ffn_b_down))
    x = x + s * g
    return x

_drawn_inputs = setup_inputs


def setup_inputs(seed=0):
    import zlib

    import numpy as np

    out = dict(_drawn_inputs(seed))
    spreads = {'L0_attn_ln1_g': (1.0, 0.2),
     'L0_attn_ln1_b': (0.0, 0.1),
     'L0_attn_b_ff1': (0.0, 0.1),
     'L0_attn_b_ff2': (0.0, 0.1),
     'L0_attn_ln2_g': (1.0, 0.2),
     'L0_attn_ln2_b': (0.0, 0.1)}
    factors = {'L0_attn_W_r': 177.495, 'L0_attn_u': 200.0, 'L0_attn_v': 188.149, 'L0_ffn_b_down': 8.0}
    for name, (base, spread) in spreads.items():
        noise = np.random.default_rng([zlib.crc32(name.encode()), seed]).standard_normal(out[name].shape)
        drawn = base * np.exp(spread * noise) if base else spread * noise
        out[name] = jnp.asarray(drawn.astype(out[name].dtype))
    for name, factor in factors.items():
        out[name] = (out[name] * factor).astype(out[name].dtype)
    return out
```

```python
from contextlib import ExitStack

import concourse.bass as bass
from concourse import mybir

LAYERS, BATCH, SEQ, D, HEADS, DH, FF = 4, 2, 1024, 128, 16, 64, 512
EXPERTS, UP = 8, 512
PAIRS = HEADS // 2
KT = SEQ // 128
HALF = 512
TOK = BATCH * SEQ
MX_TILES = 16
PROJ = [("k", 0), ("k", 1), ("q", 0), ("q", 1)]
MX_AT = [0, 0, 0, 0, 0, 0, 1, 2, 1, 2, 1, 2, 1, 2, 2, 2]
SPLIT_AT = 6
SUM_AT = 9


def build(nc, a, out_t):
    f32 = mybir.dt.float32
    f32r = mybir.dt.float32r
    ALU = mybir.AluOpType
    ACT = mybir.ActivationFunctionType
    AX = mybir.AxisListType.X
    SCALE = DH ** -0.5
    EPS = 1e-5

    ctx = ExitStack()
    with ctx:
        def sb(name, shape, dt=f32):
            return ctx.enter_context(nc.sbuf_tensor(name, shape, dt))

        def sem(name):
            return ctx.enter_context(nc.semaphore(name))

        xn_dram = nc.dram_tensor("xn_scratch", [BATCH, D, SEQ], f32).ap()
        g_dram = nc.dram_tensor("gate_scratch", [BATCH, D, SEQ], f32).ap()
        route_dram = nc.dram_tensor("route_scratch", [EXPERTS, TOK], f32).ap()
        v_dram = nc.dram_tensor("v_scratch", [KT, 128, HEADS * DH], f32).ap()
        c_dram = nc.dram_tensor("c_scratch", [HEADS, 2, SEQ], f32).ap()
        rowsum_dram = nc.dram_tensor("rowsum_scratch", [PAIRS, 2, SEQ], f32).ap()

        ident = sb("ident", [128, 128])
        r_hi = sb("r_hi", [D, SEQ], f32r)
        r_lo = sb("r_lo", [D, SEQ], f32r)
        sel = sb("sel", [2 * HEADS, PAIRS, 128], f32r)
        ones = sb("ones", [128, 64])
        zeros = sb("zeros", [128, HALF])
        hT = sb("hT", [D, SEQ])
        h_hi = sb("h_hi", [D, SEQ], f32r)
        h_lo = sb("h_lo", [D, SEQ], f32r)
        big = sb("big", [128, 8 * SEQ])
        probs = sb("probs", [128, 4, HALF])
        acc = sb("acc", [128, 2, 2, HALF])
        w_o = sb("w_o", [128, PAIRS, D])
        w_f1 = sb("w_f1", [D, FF])
        w_f2 = sb("w_f2", [128, 4, D])
        par = sb("par", [D, 9])
        q1 = sb("q1", [128, 2, 2, SEQ], f32r)
        q2 = sb("q2", [128, 2, 2, SEQ], f32r)
        k1 = sb("k1", [128, 2, 2, SEQ], f32r)
        k2 = sb("k2", [128, 2, 2, SEQ], f32r)
        qm = sb("qm", [128, 2, SEQ], f32r)
        kq_hi = sb("kq_hi", [128, 2, SEQ], f32r)
        kq_lo = sb("kq_lo", [128, 2, SEQ], f32r)
        v_slot = sb("v_slot", [128, 2, KT, 128])
        w_raw = sb("w_raw", [D, 3, 128])
        w_hi = sb("w_hi", [D, 3, 128], f32r)
        w_lo = sb("w_lo", [D, 3, 128], f32r)
        mx = sb("mx", [128, 2, 2, 4])
        m_hl = sb("m_hl", [128, 2, 2, 2, 4], f32r)
        srow = sb("srow", [128, SEQ])
        rc = sb("rc", [128, 128])
        rc_hi = sb("rc_hi", [128, 128], f32r)
        rc_lo = sb("rc_lo", [128, 128], f32r)
        rrow = sb("rrow", [2 * HEADS, SEQ], f32r)
        bst = sb("bst", [128, 4, 6])
        mv = sb("mv", [128, 4, 2])
        var4 = sb("var4", [128, 4])
        rs_l = sb("rs_l", [128, 4])
        rs_y = sb("rs_y", [128, 4])
        rs_t = sb("rs_t", [128, 3, 4])
        rstd = sb("rstd", [128, 4])
        c_hi = sb("c_hi", [HEADS, SEQ], f32r)
        c_lo = sb("c_lo", [HEADS, SEQ], f32r)
        wku = sb("wku", [D, HEADS])
        wrv = sb("wrv", [D, HEADS])
        bias_e = sb("bias_e", [128, 2, 5])
        lg = sb("lg", [128, 16, EXPERTS])
        w_rt = sb("w_rt", [D, EXPERTS])
        tie = sb("tie", [128, EXPERTS, EXPERTS])
        rt1 = sb("rt1", [128, 16, EXPERTS])
        rt2 = sb("rt2", [128, 16, EXPERTS])
        rt3 = sb("rt3", [128, 16])

        vecT = big[:, :].rearrange("p (a n) -> p a n", a=PAIRS)
        st_wv, st_wk, st_wr, st_rT, st_u, st_v, st_t0, st_t1 = (big[:, SEQ * i:SEQ * (i + 1)] for i in range(8))
        hid = big[:, 0:4 * SEQ].rearrange("p (f n) -> p f n", f=4)
        flat_acc = acc[:, :, :, :].rearrange("p a b n -> p (a b n)")
        flat_probs = probs[:, :, :].rearrange("p a n -> p (a n)")
        xT = flat_acc[:, 0:SEQ]
        yT = flat_probs[:, 0:SEQ].rearrange("p (t n) -> p t n", n=128)
        xn = big[:, 0:TOK]
        gacc = big[:, TOK:2 * TOK]
        gate_b = [big[:, TOK * (2 + i):TOK * (3 + i)] for i in range(2)]
        e_up = [w_f1[:, :], w_f2[:, :, :].rearrange("p a n -> p (a n)")]
        e_dn = [w_o[:, 0:4, :], w_o[:, 4:8, :]]
        e_h = [probs, acc[:, :, :, :].rearrange("p a b n -> p (a b) n")]
        e_tmp = v_slot[:, 0, 0:4, :].rearrange("p a n -> p (a n)")
        route_t = v_slot[0:EXPERTS, :, :, :].rearrange("p a b n -> p (a b n)")
        cmp_a = gate_b[0][:, 0:1024].rearrange("p (t e j) -> p t e j", t=16, e=EXPERTS)
        cmp_b = gate_b[0][:, 1024:2048].rearrange("p (t e j) -> p t e j", t=16, e=EXPERTS)
        sel_raw = gate_b[1][0:2 * HEADS, 0:1024]

        bank = [ctx.enter_context(nc.psum_tensor(f"bank{i}", [128, HALF], f32)) for i in range(4)]
        mxp = ctx.enter_context(nc.psum_tensor("mxp", [128, 2, HALF], f32))
        pv = ctx.enter_context(nc.psum_tensor("pv", [128, HALF], f32))
        pj = ctx.enter_context(nc.psum_tensor("pj", [128, HALF], f32))
        acc_bank = [pv, pj]

        consts = sem("consts_loaded")
        ready0 = sem("constants_ready")
        seeded = sem("semaphores_seeded")
        x_in = sem("x_loaded")
        ln_t, ln_var, ln_rs, ln_y, ln_b, ln_out = (sem(s) for s in (
            "ln_transposed", "ln_variance", "ln_rstd", "ln_normalised", "ln_back", "ln_out"))
        dve_chain, act_chain = sem("dve_chain"), sem("act_chain")
        xn_out = sem("xn_stored")
        lg_done, route_ln, route_ex, route_g, route_tr, route_cp, route_out = (sem(s) for s in (
            "logits", "route_sub", "route_exp", "route_gates", "route_transposed", "route_copied", "route_stored"))
        e_in = [sem("expert_loaded0"), sem("expert_loaded1")]
        up_done, gelu_done, down_done, mo_acc = (sem(s) for s in ("up_done", "gelu_done", "down_done", "expert_added"))
        sig, gfin, g_out = sem("sigmoid_done"), sem("gate_final"), sem("gate_stored")
        h_in = sem("h_loaded")
        layer_in, weights_in = sem("stage_a_loaded"), sem("layer_weights_loaded")
        hh_done, hl_done = sem("h_hi_done"), sem("h_lo_done")
        wc_done, wc_chain = sem("c_weights_done"), sem("c_weights_chain")
        c_mm, c_hi_done, c_lo_done, c_out = sem("c_mm"), sem("c_hi_done"), sem("c_lo_done"), sem("c_stored")
        v_mm, v_ev, v_out = sem("v_mm"), sem("v_evacuated"), [sem("v_stored0"), sem("v_stored1")]
        wraw_in, w_split, proj = sem("w_raw_loaded"), sem("w_split"), sem("projected")
        hi_done, lo_done = sem("proj_hi_done"), sem("proj_lo_done")
        dup_k, dup_q, v_in = sem("k_tiles_written"), sem("q_tiles_written"), sem("v_slot_loaded")
        m_chain, split_chain = sem("m_hi_done"), sem("w_hi_done")
        mx_mm, mx_red, m_split = sem("max_tile"), sem("max_reduced"), sem("max_split")
        m_row = [sem("m_rows0"), sem("m_rows1")]
        st_done, exp_done, pv_done = sem("scores"), sem("exps"), sem("pv_step")
        add_done = [sem("sum_added0"), sem("sum_added1")]
        pv_ev, sum_mm, sum_cp, sum_out = sem("pv_evacuated"), sem("sum_mm"), sem("sum_copied"), sem("sums_stored")
        rc_in, rc_chain, rc_done, rrow_in = sem("sums_loaded"), sem("rc_chain"), sem("rc_done"), sem("rc_rows")
        bc_mm, vec_norm, op_done, x1_done = sem("rc_broadcast"), sem("vec_normalised"), sem("out_projected"), sem("residual_done")
        f1_mm, f1_act, f2_mm, x2_done = sem("ff1_mm"), sem("ff1_act"), sem("ff2_mm"), sem("ff2_out")
        fin_in, fin_mul, fin_done, res_out = sem("final_loaded"), sem("final_mul"), sem("final_done"), sem("result_stored")
        SEEDS = [(exp_done, 4), (pv_done, 2), (add_done[0], 2), (add_done[1], 2), (sum_cp, 1), (pv_ev, 1),
                 (sum_mm, 3), (sum_out, 1), (dup_k, 1), (dup_q, 1), (mx_mm, 1), (mx_red, 1),
                 (proj, 1), (w_split, 1), (m_row[0], 1), (m_row[1], 1),
                 (mo_acc, 8), (gelu_done, 4), (down_done, 2), (fin_done, 2), (res_out, 16)]

        block = ctx.enter_context(nc.Block())

        @block.sync
        def _(sp):
            for s, k in SEEDS:
                sp.sem_inc(s, k)
            sp.sem_inc(seeded, 1)
            sp.dma_start(xT, a["xT"][:, 0:SEQ]).then_inc(x_in, 16)
            sp.dma_start(ident[:, :], a["ident"]).then_inc(consts, 16)
            sp.dma_start(w_rt[:, :], a["w_routerT"]).then_inc(consts, 16)
            sp.dma_start(tie[:, :, :], a["tie"]).then_inc(consts, 16)
            sp.dma_start(st_rT, a["rT"]).then_inc(consts, 16)
            sp.dma_start(sel_raw, a["sel"]).then_inc(consts, 16)
            sp.wait_ge(ln_t, 2)
            sp.dma_start(xT, a["xT"][:, SEQ:TOK]).then_inc(x_in, 16)
            for b in range(BATCH):
                sp.wait_ge(ln_out, 2 * (b + 1))
                sp.dma_start(xn_dram[b], xn[:, b * SEQ:(b + 1) * SEQ]).then_inc(xn_out, 16)
            sp.wait_ge(route_cp, 4)
            sp.dma_start(route_dram, route_t).then_inc(route_out, 16)
            sp.wait_ge(route_out, 16)
            sp.wait_ge(ready0, 3)
            with sp.Fori(0, EXPERTS // 2) as ep:
                for s in range(2):
                    e = ep * 2 + s
                    sp.wait_ge(mo_acc, e * 4 + 4)
                    sp.dma_start(e_up[s], a["w_upT"][e]).then_inc(e_in[s], 16)
                    sp.dma_start(e_dn[s], a["w_downT"][e].rearrange("(c p) d -> p c d", p=128)).then_inc(e_in[s], 16)
                    sp.dma_start(bias_e[:, s, :], a["bias_e"][e]).then_inc(e_in[s], 16)
                    sp.dma_start(gate_b[s], route_dram[bass.ds(e, 1), :].broadcast_to([128, TOK])).then_inc(e_in[s], 16)
            sp.wait_ge(gfin, 1)
            for b in range(BATCH):
                sp.dma_start(g_dram[b], gacc[:, b * SEQ:(b + 1) * SEQ]).then_inc(g_out, 16)
            sp.wait_ge(g_out, 16 * BATCH)
            sp.wait_ge(xn_out, 16 * BATCH)

            def load_w(m, l, p):
                sp.wait_ge(w_split, m + 1)
                sp.wait_ge(seeded, 1)
                sp.dma_start(w_raw[:, 0:2, :], a["W_qkv"][l, :, 0:2 * SEQ].rearrange(
                    "d (t a n) -> d t a n", t=2, n=128)[:, :, p, :]).then_inc(wraw_in, 16)
                sp.dma_start(w_raw[:, 2, :], a["W_r"][l].rearrange("d (a n) -> d a n", n=128)[:, p, :]).then_inc(wraw_in, 16)

            def raw(x):
                return x.bitcast(f32)

            def k_tiles(m, p, s):
                sp.wait_ge(lo_done, 4 * m + 2)
                sp.wait_ge(sum_mm, 2 * m + 1)
                for h in range(2):
                    hi, lo = (raw(x[64 * h:64 * h + 64, 0, :]) for x in (kq_hi, kq_lo))
                    sp.dma_start(raw(k1[0:64, s, h, :]), hi).then_inc(dup_k, 16)
                    sp.dma_start(raw(k1[64:128, s, h, :]), lo).then_inc(dup_k, 16)
                    sp.dma_start(raw(k2[0:64, s, h, :]), hi).then_inc(dup_k, 16)
                    sp.dma_start(raw(k2[64:66, s, h, :]), c_dram[2 * p + h]).then_inc(dup_k, 16)

            def q_tiles(m, s):
                sp.wait_ge(lo_done, 4 * m + 4)
                sp.wait_ge(mx_mm, 16 * m + 1)
                for h in range(2):
                    hi, lo = (raw(x[64 * h:64 * h + 64, 1, :]) for x in (kq_hi, kq_lo))
                    sp.dma_start(raw(qm[0:64, h, :]), hi).then_inc(dup_q, 16)
                    sp.dma_start(raw(q1[0:64, s, h, :]), hi).then_inc(dup_q, 16)
                    sp.dma_start(raw(q1[64:128, s, h, :]), hi).then_inc(dup_q, 16)
                    sp.dma_start(raw(q2[0:64, s, h, :]), lo).then_inc(dup_q, 16)

            def load_v(g, m, p, s):
                sp.dma_start(v_slot[:, s, :, :], v_dram.rearrange(
                    "t k (a n) -> k t a n", n=128)[:, :, p, :]).then_inc(v_in, 16)

            def m_rows(m, s, half):
                sp.wait_ge(m_split, 2 * m + half + 1)
                for h in range(2):
                    for i in range(2):
                        sp.dma_start(raw(q2[66 + i:67 + i, s, h, half * HALF:(half + 1) * HALF]),
                                     raw(m_hl[:, half, h, i, :])).then_inc(m_row[half], 16)

            def unit(g, l, p, s, prep, split2):
                n = g * PAIRS + p
                if split2:
                    load_w(n + 2, l, p + 2)
                if prep:
                    k_tiles(n + 1, p + 1, 1 - s)
                    q_tiles(n + 1, 1 - s)
                    load_v(g, n + 1, p + 1, 1 - s)
                    m_rows(n + 1, 1 - s, 0)
                    m_rows(n + 1, 1 - s, 1)
                sp.wait_ge(sum_cp, 2 * n + 3)
                for h in range(2):
                    sp.dma_start(rowsum_dram.rearrange("a h n -> h a n")[h, p, :], srow[64 * h:64 * h + 1, :]).then_inc(sum_out, 16)

            with sp.Fori(0, BATCH) as b:
                sp.wait_ge(res_out, 16 * b + 16)
                sp.wait_ge(fin_done, 2 * b + 2)
                sp.dma_start(hT[:, :], xn_dram[b]).then_inc(h_in, 16)
                with sp.Fori(0, LAYERS) as l:
                    g = b * LAYERS + l
                    sp.wait_ge(ln_out, 4 * g + 4)
                    load_w(g * PAIRS, l, 0)
                    sp.dma_start(st_wk, a["W_qkv"][l, :, SEQ:2 * SEQ]).then_inc(layer_in, 16)
                    sp.dma_start(st_wr, a["W_r"][l]).then_inc(layer_in, 16)
                    sp.dma_start(st_u, a["u"].broadcast_to([128, SEQ])).then_inc(layer_in, 16)
                    sp.dma_start(st_v, a["v"].broadcast_to([128, SEQ])).then_inc(layer_in, 16)
                    sp.dma_start(st_rT, a["rT"]).then_inc(layer_in, 16)
                    sp.dma_start(st_wv, a["W_qkv"][l, :, 2 * SEQ:3 * SEQ]).then_inc(layer_in, 16)
                    sp.dma_start(w_o[:, :, :], a["W_o"][l].rearrange("(a p) d -> p a d", p=128)).then_inc(weights_in, 16)
                    sp.dma_start(w_f1[:, :], a["W_ff1"][l]).then_inc(weights_in, 16)
                    sp.dma_start(w_f2[:, :, :], a["W_ff2"][l].rearrange("(c p) d -> p c d", p=128)).then_inc(weights_in, 16)
                    sp.dma_start(par[:, :], a["par"][l]).then_inc(weights_in, 16)
                    load_w(g * PAIRS + 1, l, 1)
                    sp.wait_ge(c_lo_done, 2 * g + 2)
                    sp.wait_ge(c_hi_done, 2 * g + 2)
                    sp.dma_start(c_dram[:, 0, :], raw(c_hi[:, :])).then_inc(c_out, 16)
                    sp.dma_start(c_dram[:, 1, :], raw(c_lo[:, :])).then_inc(c_out, 16)
                    sp.wait_ge(c_out, 32 * g + 32)
                    k_tiles(g * PAIRS, 0, 0)
                    q_tiles(g * PAIRS, 0)
                    m_rows(g * PAIRS, 0, 0)
                    for i in range(2):
                        sp.wait_ge(v_out[i], 64 * g + 64)
                    load_v(g, g * PAIRS, 0, 0)
                    m_rows(g * PAIRS, 0, 1)
                    with sp.Fori(0, PAIRS // 2 - 1) as j:
                        unit(g, l, j * 2, 0, True, True)
                        unit(g, l, j * 2 + 1, 1, True, True)
                    unit(g, l, PAIRS - 2, 0, True, False)
                    unit(g, l, PAIRS - 1, 1, False, False)
                    sp.wait_ge(sum_out, 32 * PAIRS * (g + 1) + 1)
                    sp.dma_start(rc[:, :], rowsum_dram.rearrange("a h (c n) -> (a h c) n", n=128)).then_inc(rc_in, 16)
                    sp.wait_ge(rc_done, g + 1)
                    sp.dma_start(raw(rrow[0:HEADS, :]), raw(rc_hi[:, :])).then_inc(rrow_in, 16)
                    sp.dma_start(raw(rrow[HEADS:2 * HEADS, :]), raw(rc_lo[:, :])).then_inc(rrow_in, 16)
                sp.wait_ge(ln_out, 4 * b * LAYERS + 4 * LAYERS + 4)
                sp.dma_start(st_wv, a["xT"].rearrange("d (b n) -> d b n", b=BATCH)[:, b, :]).then_inc(fin_in, 16)
                sp.dma_start(st_wk, g_dram[b]).then_inc(fin_in, 16)
                sp.wait_ge(fin_done, 2 * b + 4)
                sp.dma_start(out_t.rearrange("d (b n) -> d b n", b=BATCH)[:, b, :], st_t0).then_inc(res_out, 16)
            sp.wait_ge(res_out, BATCH * 16 + 16)

        @block.tensor
        def _(pe):
            def ln(H, half):
                for i in range(4):
                    t = half * 4 + i
                    last = nc.tensor.transpose(mxp[:, half, i * 128:(i + 1) * 128], xT[:, t * 128:(t + 1) * 128], ident[:, :])
                last.then_inc(ln_t, 1)

            def ln_back(H, half):
                pe.wait_ge(ln_y, H + 1)
                for i in range(4):
                    last = nc.tensor.transpose(mxp[:, half, i * 128:(i + 1) * 128], yT[:, half * 4 + i, :], ident[:, :])
                last.then_inc(ln_b, 1)

            pe.wait_ge(seeded, 1)
            pe.wait_ge(consts, 80)
            for b in range(BATCH):
                pe.wait_ge(x_in, 16 * (b + 1))
                for half in range(2):
                    if b:
                        pe.wait_ge(ln_out, half + 1)
                    ln(2 * b + half, half)
                for half in range(2):
                    ln_back(2 * b + half, half)
            pe.wait_ge(ln_out, 4)
            for t in range(16):
                last = nc.tensor.matmul(mxp[:, 0, t * EXPERTS:(t + 1) * EXPERTS], xn[:, t * 128:(t + 1) * 128],
                                        w_rt[:, :], start=True, stop=True)
            last.then_inc(lg_done, 1)
            pe.wait_ge(route_g, 1)
            for t in range(16):
                last = nc.tensor.transpose(bank[t // 4][0:EXPERTS, (t % 4) * 128:(t % 4 + 1) * 128], lg[:, t, :], ident[:, :])
                if t % 4 == 3:
                    last.then_inc(route_tr, 1)
            pe.wait_ge(route_cp, 4)

            with pe.Fori(0, EXPERTS // 2) as ep:
                for s in range(2):
                    e = ep * 2 + s

                    def up(tc):
                        for f in range(4):
                            pe.wait_ge(gelu_done, (e * 4 + tc) * 4 + f + 1)
                            nc.tensor.matmul(bank[f][:, :], e_up[s][:, f * 128:(f + 1) * 128],
                                             xn[:, tc * HALF:(tc + 1) * HALF], start=True, stop=True).then_inc(up_done, 1)

                    def down(tc):
                        pe.wait_ge(mo_acc, e * 4 + tc + 7)
                        pe.wait_ge(gelu_done, (e * 4 + tc) * 4 + 8)
                        for f in range(4):
                            last = nc.tensor.matmul(acc_bank[tc % 2][:, :], e_dn[s][:, f, :], e_h[tc % 2][:, f, :],
                                                    start=(f == 0), stop=(f == 3))
                        last.then_inc(down_done, 1)

                    pe.wait_ge(e_in[s], ep * 64 + 64)
                    up(0)
                    for tc in range(4):
                        if tc < 3:
                            up(tc + 1)
                        down(tc)

            def project(m, i):
                kind, c = PROJ[i]
                if i:
                    pe.wait_ge(lo_done, 4 * m + i)
                cols = slice(c * HALF, (c + 1) * HALF)
                w = 1 if kind == "k" else 0
                ops = [(w_hi, w, h_hi), (w_hi, w, h_lo), (w_lo, w, h_hi)]
                if kind == "k":
                    ops += [(w_hi, 2, r_hi), (w_hi, 2, r_lo), (w_lo, 2, r_hi)]
                for j, (wt, k, x) in enumerate(ops):
                    last = nc.tensor.matmul(pj[:, :], wt[:, k, :], x[:, cols], start=(j == 0), stop=(j == len(ops) - 1))
                last.then_inc(proj, 1)

            def max_tile(m, s, t):
                if t == 0:
                    pe.wait_ge(dup_k, 128 * m + 129)
                    pe.wait_ge(dup_q, 128 * m + 129)
                half, h, j = t // 8, t // 4 % 2, t % 4
                pe.wait_ge(mx_red, 16 * m + t + 1)
                w = qm[0:66, h, half * HALF:(half + 1) * HALF].rearrange("p (q j) -> p j q", j=4)[:, j, :]
                for c in range(2):
                    last = nc.tensor.matmul(mxp[:, c, :], w, k2[0:66, s, h, c * HALF:(c + 1) * HALF], start=True, stop=True)
                last.then_inc(mx_mm, 1)

            def scores(n, s, i):
                half, kt, h = i // 16, i // 2 % 8, i % 2
                if i % 16 == 0:
                    pe.wait_ge(m_row[half], 64 * n + 65)
                pe.wait_ge(exp_done, 32 * n + i + 1)
                ks, qs = slice(kt * 128, (kt + 1) * 128), slice(half * HALF, (half + 1) * HALF)
                nc.tensor.matmul(bank[i % 4][:, :], k1[:, s, h, ks], q1[:, s, h, qs], start=True, stop=False)
                nc.tensor.matmul(bank[i % 4][:, :], k2[0:68, s, h, ks], q2[0:68, s, h, qs],
                                 start=False, stop=True).then_inc(st_done, 1)

            def sums(n, half):
                for h in range(2):
                    pe.wait_ge(add_done[h], 16 * n + 8 * half + 10)
                    last = nc.tensor.matmul(pj[64 * h:64 * h + 64, :], ones[:, :], acc[:, half, h, :], start=True, stop=True)
                last.then_inc(sum_mm, 1)

            def unit(g, p, s, prep):
                n = g * PAIRS + p
                t = 0
                for step in range(16):
                    half, kt = step // 8, step % 8
                    if prep and step == 0:
                        pe.wait_ge(w_split, n + 3)
                        pe.wait_ge(sum_cp, 2 * n + 1)
                    if prep and step < 4:
                        project(n + 1, step)
                    if prep and MX_AT[step] > 1:
                        max_tile(n + 1, 1 - s, t)
                        t += 1
                    if step < 15:
                        scores(n, s, 2 * step + 2)
                        scores(n, s, 2 * step + 3)
                    elif prep:
                        scores(n + 1, 1 - s, 0)
                        scores(n + 1, 1 - s, 1)
                    if prep and MX_AT[step] > 0:
                        max_tile(n + 1, 1 - s, t)
                        t += 1
                    if kt == 0:
                        pe.wait_ge(pv_ev, 2 * n + half + 1)
                    if step == 0:
                        pe.wait_ge(v_in, 16 * n + 16)
                    for h in range(2):
                        i = 2 * step + h
                        pe.wait_ge(exp_done, 32 * n + i + 5)
                        last = nc.tensor.matmul(pv[64 * h:64 * h + 64, :], v_slot[:, s, kt, 64 * h:64 * h + 64],
                                                probs[:, i % 4, :], start=(kt == 0), stop=(kt == 7))
                    last.then_inc(pv_done, 1)
                    if step == SUM_AT:
                        if prep:
                            pe.wait_ge(lo_done, 4 * n + 8)
                        pe.wait_ge(sum_cp, 2 * n + 1)
                        sums(n, 0)
                pe.wait_ge(sum_cp, 2 * n + 2)
                sums(n, 1)

            with pe.Fori(0, BATCH) as b:
                with pe.Fori(0, LAYERS) as l:
                    g = b * LAYERS + l
                    n0 = g * PAIRS
                    pe.wait_ge(ln_out, 4 * g + 4)
                    pe.wait_ge(hh_done, g + 1)
                    pe.wait_ge(hl_done, g + 1)
                    pe.wait_ge(w_split, n0 + 2)
                    for i in range(4):
                        project(n0, i)
                        if i == 1:
                            pe.wait_ge(wc_done, g + 1)
                            for half in range(2):
                                hs = slice(half * HALF, (half + 1) * HALF)
                                nc.tensor.matmul(bank[half][0:HEADS, :], wku[:, :], hT[:, hs], start=True, stop=False)
                                nc.tensor.matmul(bank[half][0:HEADS, :], wrv[:, :], st_rT[:, hs], start=False, stop=True)\
                                    .then_inc(c_mm, 1)
                    pe.wait_ge(layer_in, 96 * g + 96)
                    t = 0
                    for i in range(16):
                        if i >= 4:
                            pe.wait_ge(v_ev, 16 * g + i - 3)
                        b_i = (i + 2) % 4
                        if i in (2, 3):
                            pe.wait_ge(c_lo_done, 2 * g + i - 1)
                        nc.tensor.matmul(bank[b_i][:, :], hT[:, (i // 2) * 128:(i // 2 + 1) * 128],
                                         st_wv[:, (i % 2) * HALF:(i % 2 + 1) * HALF], start=True, stop=True).then_inc(v_mm, 1)
                        if i >= 6:
                            max_tile(n0, 0, t)
                            t += 1
                    while t < MX_TILES:
                        max_tile(n0, 0, t)
                        t += 1
                    pe.wait_ge(v_ev, 16 * g + 16)
                    scores(n0, 0, 0)
                    scores(n0, 0, 1)
                    with pe.Fori(0, PAIRS // 2 - 1) as j:
                        unit(g, j * 2, 0, True)
                        unit(g, j * 2 + 1, 1, True)
                    unit(g, PAIRS - 2, 0, True)
                    unit(g, PAIRS - 1, 1, False)
                    pe.wait_ge(rrow_in, 32 * g + 32)
                    pe.wait_ge(weights_in, 64 * g + 64)
                    pe.wait_ge(exp_done, 32 * (n0 + PAIRS) + 4)
                    pe.wait_ge(sum_cp, 2 * (n0 + PAIRS) + 1)
                    pe.wait_ge(pv_ev, 2 * (n0 + PAIRS) + 1)
                    for i in range(2 * PAIRS + 3):
                        if i < 2 * PAIRS:
                            if i >= 4:
                                pe.wait_ge(vec_norm, 2 * PAIRS * g + i - 3)
                            nc.tensor.matmul(bank[i % 4][:, :], sel[:, i // 2, :], rrow[:, (i % 2) * HALF:(i % 2 + 1) * HALF],
                                             start=True, stop=True).then_inc(bc_mm, 1)
                        if i >= 3:
                            o = i - 3
                            pe.wait_ge(vec_norm, 2 * PAIRS * g + o + 1)
                            last = nc.tensor.matmul(acc_bank[o % 2][:, :], w_o[:, o // 2, :],
                                                    vecT[:, o // 2, (o % 2) * HALF:(o % 2 + 1) * HALF],
                                                    start=(o < 2), stop=(o >= 2 * PAIRS - 2))
                            if o >= 2 * PAIRS - 2:
                                last.then_inc(op_done, 1)
                    H = 4 * g + 4
                    for half in range(2):
                        pe.wait_ge(x1_done, 2 * g + half + 1)
                        ln(H + half, half)
                    for half in range(2):
                        ln_back(H + half, half)
                        pe.wait_ge(ln_out, H + half + 1)
                        hs = slice(half * HALF, (half + 1) * HALF)
                        for f in range(4):
                            if half:
                                pe.wait_ge(f1_act, 8 * g + f + 1)
                            nc.tensor.matmul(bank[f][:, :], w_f1[:, f * 128:(f + 1) * 128], hT[:, hs], start=True, stop=True)\
                                .then_inc(f1_mm, 1)
                    for half in range(2):
                        pe.wait_ge(f1_act, 8 * g + 4 * half + 4)
                        hs = slice(half * HALF, (half + 1) * HALF)
                        for f in range(4):
                            last = nc.tensor.matmul(acc_bank[half][:, :], w_f2[:, f, :], hid[:, f, hs], start=(f == 0), stop=(f == 3))
                        last.then_inc(f2_mm, 1)
                    for half in range(2):
                        pe.wait_ge(x2_done, 2 * g + half + 1)
                        ln(H + 2 + half, half)
                    for half in range(2):
                        ln_back(H + 2 + half, half)

        @block.scalar
        def _(act):
            def ln(H, half, out, scale=1.0, bias=0.0):
                act.wait_ge(ln_var, H + 1)
                nc.scalar.activation(rs_l[:, :], var4[:, :], ACT.Ln).then_inc(act_chain, 1)
                act.wait_ge(act_chain, H + 1)
                nc.scalar.activation(rs_y[:, :], rs_l[:, :], ACT.Exp, scale=-0.5).then_inc(ln_rs, 1)

            def ln_finish(H, half, out, scale=1.0, bias=0.0):
                act.wait_ge(ln_b, H + 1)
                nc.scalar.activation(out, mxp[:, half, :], ACT.Identity, scale=scale, bias=bias).then_inc(ln_out, 1)

            act.wait_ge(seeded, 1)
            act.wait_ge(consts, 80)
            nc.scalar.activation(r_hi[:, :], st_rT, ACT.Copy).then_inc(ready0, 1)
            for b in range(BATCH):
                for half in range(2):
                    ln(2 * b + half, half, None)
                for half in range(2):
                    ln_finish(2 * b + half, half, xn[:, b * SEQ + half * HALF:b * SEQ + (half + 1) * HALF])
            act.wait_ge(route_ln, 1)
            nc.scalar.activation(rt1[:, :, :], rt1[:, :, :], ACT.Exp).then_inc(route_ex, 1)
            for i in range(4):
                act.wait_ge(route_tr, i + 1)
                nc.scalar.activation(route_t[:, i * HALF:(i + 1) * HALF], bank[i][0:EXPERTS, :], ACT.Copy).then_inc(route_cp, 1)
            with act.Fori(0, EXPERTS // 2) as ep:
                for s in range(2):
                    e = ep * 2 + s
                    act.wait_ge(e_in[s], ep * 64 + 64)
                    for tc in range(4):
                        act.wait_ge(down_done, e * 4 + tc + 1)
                        for f in range(4):
                            act.wait_ge(up_done, (e * 4 + tc) * 4 + f + 1)
                            nc.scalar.activation(e_h[tc % 2][:, f, :], bank[f][:, :], ACT.Gelu,
                                                 bias=bias_e[:, s, f:f + 1]).then_inc(gelu_done, 1)
            act.wait_ge(mo_acc, 4 * EXPERTS + 8)
            nc.scalar.activation(gate_b[0], gacc, ACT.Sigmoid).then_inc(sig, 1)

            def hi_half(m, i):
                kq, c = i // 2, i % 2
                if i % 2 == 0:
                    act.wait_ge((dup_k, dup_q)[kq], 128 * m + 1)
                act.wait_ge(proj, 4 * m + i + 2)
                nc.scalar.activation(kq_hi[:, kq, c * HALF:(c + 1) * HALF], pj[:, :], ACT.Copy).then_inc(hi_done, 1)

            def unit(g, p, s, prep):
                n = g * PAIRS + p
                for step in range(16):
                    half, kt = step // 8, step % 8
                    act.wait_ge(pv_done, 16 * n + step + 1)
                    for h in range(2):
                        act.wait_ge(add_done[h], 16 * n + step + 1)
                        i = 2 * step + h
                        act.wait_ge(st_done, 32 * n + i + 1)
                        nc.scalar.activation(probs[:, i % 4, :], bank[i % 4][:, :], ACT.Exp, scale=SCALE).then_inc(exp_done, 1)
                    if prep and step < 4:
                        hi_half(n + 1, step)
                    if step == SUM_AT:
                        sum_copy(n, 0)
                    if kt == 7:
                        act.wait_ge(pv_done, 16 * n + step + 3)
                        nc.scalar.activation(big[:, bass.ds(p * SEQ + half * HALF, HALF)],
                                             pv[:, :], ACT.Copy).then_inc(pv_ev, 1)
                sum_copy(n, 1)

            def sum_copy(n, half):
                act.wait_ge(sum_mm, 2 * n + half + 4)
                if half == 0:
                    act.wait_ge(sum_out, 32 * n + 1)
                nc.scalar.activation(srow[:, half * HALF:(half + 1) * HALF], pj[:, :], ACT.Copy).then_inc(sum_cp, 1)

            with act.Fori(0, BATCH) as b:
                with act.Fori(0, LAYERS) as l:
                    g = b * LAYERS + l
                    n0 = g * PAIRS
                    act.wait_ge(h_in, b * 16 + 16)
                    act.wait_ge(ln_out, 4 * g + 4)
                    nc.scalar.activation(h_hi[:, :], hT[:, :], ACT.Copy).then_inc(hh_done, 1)
                    for i in range(2):
                        hi_half(n0, i)
                    for half in range(2):
                        act.wait_ge(c_mm, 2 * g + half + 1)
                        nc.scalar.activation(c_hi[:, half * HALF:(half + 1) * HALF], bank[half][0:HEADS, :], ACT.Copy)\
                            .then_inc(c_hi_done, 1)
                    for i in range(2, 4):
                        hi_half(n0, i)
                    for i in range(16):
                        t, c = i // 2, i % 2
                        act.wait_ge(v_mm, 16 * g + i + 1)
                        if i >= 4 and c == 0:
                            act.wait_ge(v_out[t % 2], 64 * g + 16 * (t // 2))
                        nc.scalar.activation((st_t0, st_t1)[t % 2][:, c * HALF:(c + 1) * HALF], bank[(i + 2) % 4][:, :],
                                             ACT.Copy).then_inc(v_ev, 1)
                        if c:
                            act.wait_ge(v_ev, 16 * g + i + 1)
                            act.dma_start(v_dram[t], (st_t0, st_t1)[t % 2]).then_inc(v_out[t % 2], 16)
                    with act.Fori(0, PAIRS // 2 - 1) as j:
                        unit(g, j * 2, 0, True)
                        unit(g, j * 2 + 1, 1, True)
                    unit(g, PAIRS - 2, 0, True)
                    unit(g, PAIRS - 1, 1, False)
                    H = 4 * g + 4
                    act.wait_ge(weights_in, 64 * g + 64)
                    for half in range(2):
                        ln(H + half, half, None)
                    for half in range(2):
                        hs = slice(half * HALF, (half + 1) * HALF)
                        ln_finish(H + half, half, hT[:, hs], par[:, 0:1], par[:, 1:2])
                        for f in range(4):
                            act.wait_ge(f1_mm, 8 * g + 4 * half + f + 1)
                            nc.scalar.activation(hid[:, f, hs], bank[f][:, :], ACT.Relu, bias=par[:, 5 + f:6 + f])\
                                .then_inc(f1_act, 1)
                    for half in range(2):
                        hs = slice(half * HALF, (half + 1) * HALF)
                        act.wait_ge(f2_mm, 2 * g + half + 1)
                        nc.scalar.activation(xT[:, hs], acc_bank[half][:, :], ACT.Identity, bias=par[:, 4:5]).then_inc(x2_done, 1)
                    for half in range(2):
                        ln(H + 2 + half, half, None)
                    for half in range(2):
                        hs = slice(half * HALF, (half + 1) * HALF)
                        ln_finish(H + 2 + half, half, hT[:, hs], par[:, 2:3], par[:, 3:4])

        @block.vector
        def _(dve):
            def ln(H, half, chain):
                def link(ins, k):
                    ins.then_inc(dve_chain, 1)
                    dve.wait_ge(dve_chain, H * 6 + k)
                dve.wait_ge(ln_t, H + 1)
                for i in range(4):
                    last = nc.vector.bn_stats(bst[:, i, :], mxp[:, half, i * 128:(i + 1) * 128])
                link(last, 1)
                nc.vector.memset(rs_t[:, 2, :], 0.0)
                for i in range(4):
                    last = nc.vector.bn_aggr(mv[:, i, :], bst[:, i, :])
                link(last, 2)
                nc.vector.tensor_scalar(var4[:, :], mv[:, :, 1], EPS, None, ALU.add).then_inc(ln_var, 1)
                dve.wait_ge(ln_var, H + 1)
                dve.wait_ge(ln_rs, H + 1)
                link(nc.vector.tensor_tensor(rs_t[:, 0, :], rs_y[:, :], rs_y[:, :], ALU.mult), 3)
                link(nc.vector.tensor_tensor(rs_t[:, 1, :], rs_t[:, 0, :], var4[:, :], ALU.mult), 4)
                link(nc.vector.tensor_scalar(rs_t[:, 0, :], rs_t[:, 1, :], -0.5, 1.5, ALU.mult, ALU.add), 5)
                link(nc.vector.tensor_tensor(rstd[:, :], rs_y[:, :], rs_t[:, 0, :], ALU.mult), 6)
                for i in range(4):
                    last = nc.vector.tensor_scalar(yT[:, half * 4 + i, :], mxp[:, half, i * 128:(i + 1) * 128],
                                                   mv[:, i, 0:1], rstd[:, i:i + 1], ALU.subtract, ALU.mult)
                last.then_inc(ln_y, 1)

            dve.wait_ge(seeded, 1)
            nc.vector.memset(ones[:, :], 1.0)
            for x in (q2, k2):
                nc.vector.memset(x[64:128, :, :, :].bitcast(f32), 1.0)
            nc.vector.memset(qm[64:128, :, :].bitcast(f32), 1.0)
            nc.vector.memset(zeros[:, :], 0.0).then_inc(ready0, 1)
            dve.wait_ge(consts, 80)
            nc.vector.tensor_copy(sel[:, :, :].rearrange("p a n -> p (a n)"), sel_raw)
            dve.wait_ge(ready0, 2)
            nc.vector.tensor_tensor(r_lo[:, :], st_rT, r_hi[:, :].bitcast(f32), ALU.subtract).then_inc(ready0, 1)
            for b in range(BATCH):
                for half in range(2):
                    ln(2 * b + half, half, None)
            dve.wait_ge(ready0, 3)
            dve.wait_ge(lg_done, 1)
            rch = [0]

            def rlink(ins):
                rch[0] += 1
                ins.then_inc(wc_chain, 1)
                dve.wait_ge(wc_chain, rch[0])

            rlink(nc.vector.tensor_copy(lg[:, :, :].rearrange("p t e -> p (t e)"), mxp[:, 0, 0:16 * EXPERTS]))
            l_j = lg[:, :, :].unsqueeze(2).broadcast_to([128, 16, EXPERTS, EXPERTS])
            l_e = lg[:, :, :].unsqueeze(3).broadcast_to([128, 16, EXPERTS, EXPERTS])
            nc.vector.reduce_max(rt3[:, :], lg[:, :, :], AX)
            nc.vector.tensor_tensor(cmp_a, l_j, l_e, ALU.is_equal)
            rlink(nc.vector.tensor_tensor(cmp_b, l_j, l_e, ALU.is_gt))
            rlink(nc.vector.tensor_tensor(cmp_a, cmp_a, tie[:, :, :].unsqueeze(1).broadcast_to([128, 16, EXPERTS, EXPERTS]), ALU.mult))
            rlink(nc.vector.tensor_tensor(cmp_a, cmp_a, cmp_b, ALU.add))
            rlink(nc.vector.tensor_reduce(rt2[:, :, :], cmp_a, AX, ALU.add))
            rlink(nc.vector.tensor_scalar(rt2[:, :, :], rt2[:, :, :], 2.0, None, ALU.is_lt))
            nc.vector.tensor_tensor(rt1[:, :, :], lg[:, :, :], rt3[:, :].unsqueeze(2).broadcast_to([128, 16, EXPERTS]),
                                    ALU.subtract).then_inc(route_ln, 1)
            dve.wait_ge(route_ex, 1)
            rlink(nc.vector.tensor_tensor(rt2[:, :, :], rt2[:, :, :], rt1[:, :, :], ALU.mult))
            rlink(nc.vector.reduce_sum(rt3[:, :], rt2[:, :, :], AX))
            rlink(nc.vector.reciprocal(rt3[:, :], rt3[:, :]))
            nc.vector.tensor_tensor(lg[:, :, :], rt2[:, :, :], rt3[:, :].unsqueeze(2).broadcast_to([128, 16, EXPERTS]),
                                    ALU.mult).then_inc(route_g, 1)
            rlink(nc.vector.memset(gacc, 0.0))
            RC = rch[0]
            with dve.Fori(0, EXPERTS // 2) as ep:
                for s in range(2):
                    e = ep * 2 + s
                    dve.wait_ge(e_in[s], ep * 64 + 64)
                    for tc in range(4):
                        ts = slice(tc * HALF, (tc + 1) * HALF)
                        dve.wait_ge(down_done, e * 4 + tc + 3)
                        dve.wait_ge(mo_acc, e * 4 + tc + 8)
                        nc.vector.scalar_tensor_tensor(e_tmp, acc_bank[tc % 2][:, :], bias_e[:, s, 4:5], gate_b[s][:, ts],
                                                       op0=ALU.add, op1=ALU.mult).then_inc(wc_chain, 1)
                        dve.wait_ge(wc_chain, e * 4 + tc + RC + 1)
                        nc.vector.tensor_tensor(gacc[:, ts], gacc[:, ts], e_tmp, ALU.add).then_inc(mo_acc, 1)
            dve.wait_ge(sig, 1)
            nc.vector.tensor_tensor(gacc, gacc, gate_b[0], ALU.mult).then_inc(gfin, 1)
            WC0 = RC + 4 * EXPERTS

            def lo_half(m, i):
                kq, c = i // 2, i % 2
                cs = slice(c * HALF, (c + 1) * HALF)
                dve.wait_ge(hi_done, 4 * m + i + 1)
                nc.vector.tensor_tensor(kq_lo[:, kq, cs], pj[:, :], kq_hi[:, kq, cs].bitcast(f32), ALU.subtract)\
                    .then_inc(lo_done, 1)

            def max_reduce(m, t):
                half, h, j = t // 8, t // 4 % 2, t % 4
                dve.wait_ge(mx_mm, 16 * m + t + 2)
                nc.vector.reduce_max(mx[:, half, h, j:j + 1], mxp[:, :, :].rearrange("p c n -> p (c n)"), AX).then_inc(mx_red, 1)
                if t % 8 == 7:
                    dve.wait_ge(mx_red, 16 * m + t + 2)
                    dve.wait_ge(m_row[half], 64 * m + 1)
                    nc.vector.tensor_scalar(m_hl[:, half, :, 0, :], mx[:, half, :, :], -1.0, None, ALU.mult).then_inc(m_chain, 1)
                    dve.wait_ge(m_chain, 2 * m + half + 1)
                    nc.vector.scalar_tensor_tensor(m_hl[:, half, :, 1, :], mx[:, half, :, :], -1.0,
                                                   m_hl[:, half, :, 0, :].bitcast(f32), op0=ALU.mult,
                                                   op1=ALU.subtract).then_inc(m_split, 1)

            def unit(g, p, s, prep):
                n = g * PAIRS + p
                t = 0
                for step in range(16):
                    half, kt = step // 8, step % 8
                    if prep and MX_AT[step] > 1:
                        max_reduce(n + 1, t)
                        t += 1
                    if prep and MX_AT[step] > 0:
                        max_reduce(n + 1, t)
                        t += 1
                    dve.wait_ge(exp_done, 32 * n + 2 * step + 5)
                    pr, ac = probs[:, 2 * step % 4, :], acc[:, half, 0, :]
                    if kt == 0:
                        dve.wait_ge(sum_mm, 2 * n + half + 2)
                        nc.vector.tensor_copy(ac, pr).then_inc(add_done[0], 1)
                    else:
                        dve.wait_ge(add_done[0], 16 * n + step + 2)
                        nc.vector.tensor_tensor(ac, ac, pr, ALU.add).then_inc(add_done[0], 1)
                    if prep and step < 4:
                        lo_half(n + 1, step)

            with dve.Fori(0, BATCH) as b:
                with dve.Fori(0, LAYERS) as l:
                    g = b * LAYERS + l
                    n0 = g * PAIRS
                    dve.wait_ge(hh_done, g + 1)
                    nc.vector.tensor_tensor(h_lo[:, :], hT[:, :], h_hi[:, :].bitcast(f32), ALU.subtract).then_inc(hl_done, 1)
                    dve.wait_ge(layer_in, 96 * g + 96)
                    for i, (w, uv, o) in enumerate(((st_wk, st_u, wku), (st_wr, st_v, wrv))):
                        nc.vector.tensor_tensor((st_t0, st_t1)[i], w, uv, ALU.mult).then_inc(wc_chain, 1)
                        dve.wait_ge(wc_chain, WC0 + 2 * g + i + 1)
                        last = nc.vector.tensor_reduce(o[:, :], (st_t0, st_t1)[i].rearrange("p (h d) -> p h d", d=DH), AX, ALU.add)
                    last.then_inc(wc_done, 1)
                    for i in range(2):
                        lo_half(n0, i)
                    for half in range(2):
                        dve.wait_ge(c_hi_done, 2 * g + half + 1)
                        hs = slice(half * HALF, (half + 1) * HALF)
                        nc.vector.tensor_tensor(c_lo[:, hs], bank[half][0:HEADS, :], c_hi[:, hs].bitcast(f32), ALU.subtract)\
                            .then_inc(c_lo_done, 1)
                    for i in range(2, 4):
                        lo_half(n0, i)
                    for t in range(MX_TILES):
                        max_reduce(n0, t)
                    with dve.Fori(0, PAIRS // 2 - 1) as j:
                        unit(g, j * 2, 0, True)
                        unit(g, j * 2 + 1, 1, True)
                    unit(g, PAIRS - 2, 0, True)
                    unit(g, PAIRS - 1, 1, False)
                    dve.wait_ge(rc_in, 16 * g + 16)
                    nc.vector.reciprocal(rc[:, :], rc[:, :]).then_inc(rc_chain, 1)
                    dve.wait_ge(rc_chain, 2 * g + 1)
                    nc.vector.tensor_copy(rc_hi[:, :], rc[:, :]).then_inc(rc_chain, 1)
                    dve.wait_ge(rc_chain, 2 * g + 2)
                    nc.vector.tensor_tensor(rc_lo[:, :], rc[:, :], rc_hi[:, :].bitcast(f32), ALU.subtract).then_inc(rc_done, 1)
                    dve.wait_ge(pv_ev, 2 * (n0 + PAIRS) + 1)
                    for i in range(2 * PAIRS):
                        v = vecT[:, i // 2, (i % 2) * HALF:(i % 2 + 1) * HALF]
                        dve.wait_ge(bc_mm, 2 * PAIRS * g + i + 1)
                        nc.vector.tensor_tensor(v, bank[i % 4][:, :], v, ALU.mult).then_inc(vec_norm, 1)
                    for half in range(2):
                        hs = slice(half * HALF, (half + 1) * HALF)
                        dve.wait_ge(op_done, 2 * g + half + 1)
                        nc.vector.tensor_tensor(xT[:, hs], acc_bank[half][:, :], hT[:, hs], ALU.add).then_inc(x1_done, 1)
                    for k in range(2):
                        for half in range(2):
                            ln(4 * g + 4 + 2 * k + half, half, None)
                dve.wait_ge(ln_out, 4 * b * LAYERS + 4 * LAYERS + 4)
                dve.wait_ge(fin_in, b * 32 + 32)
                nc.vector.tensor_tensor(st_t0, hT[:, :], st_wk, ALU.mult).then_inc(fin_done, 1)
                dve.wait_ge(fin_done, 2 * b + 3)
                nc.vector.tensor_tensor(st_t0, st_t0, st_wv, ALU.add).then_inc(fin_done, 1)

        @block.gpsimd
        def _(pool):
            pool.wait_ge(seeded, 1)
            pool.wait_ge(ready0, 3)

            def split_w(m):
                pool.wait_ge(wraw_in, 32 * m + 32)
                pool.wait_ge(proj, 4 * m + 1)
                nc.gpsimd.tensor_tensor(w_hi[:, :, :], w_raw[:, :, :], zeros[:, 0:384].rearrange("p (a n) -> p a n", a=3),
                                        ALU.add).then_inc(split_chain, 1)
                pool.wait_ge(split_chain, m + 1)
                nc.gpsimd.tensor_tensor(w_lo[:, :, :], w_raw[:, :, :], w_hi[:, :, :].bitcast(f32), ALU.subtract)\
                    .then_inc(w_split, 1)

            def unit(g, p, s, split2):
                n = g * PAIRS + p
                for step in range(16):
                    half, kt = step // 8, step % 8
                    pool.wait_ge(exp_done, 32 * n + 2 * step + 6)
                    pr, ac = probs[:, (2 * step + 1) % 4, :], acc[:, half, 1, :]
                    if kt == 0:
                        pool.wait_ge(sum_mm, 2 * n + half + 2)
                        nc.gpsimd.tensor_tensor(ac, pr, zeros[:, :], ALU.add).then_inc(add_done[1], 1)
                    else:
                        pool.wait_ge(add_done[1], 16 * n + step + 2)
                        nc.gpsimd.tensor_tensor(ac, ac, pr, ALU.add).then_inc(add_done[1], 1)
                    if split2 and step == SPLIT_AT:
                        split_w(n + 2)

            with pool.Fori(0, BATCH) as b:
                with pool.Fori(0, LAYERS) as l:
                    g = b * LAYERS + l
                    split_w(g * PAIRS)
                    split_w(g * PAIRS + 1)
                    with pool.Fori(0, PAIRS // 2 - 1) as j:
                        unit(g, j * 2, 0, True)
                        unit(g, j * 2 + 1, 1, True)
                    unit(g, PAIRS - 2, 0, False)
                    unit(g, PAIRS - 1, 1, False)


def position_encoding(np):
    pos = np.arange(SEQ - 1, -1, -1, dtype=np.float32)
    freq = np.float32(1.0) / np.power(np.float32(10000.0), np.arange(0, D, 2, dtype=np.float32) / np.float32(D))
    ang = pos[:, None] * freq[None, :].astype(np.float32)
    return np.ascontiguousarray(np.concatenate([np.sin(ang), np.cos(ang)], axis=-1).T.astype(np.float32))


def kernel(**inputs):
    import numpy as np
    import concourse.bacc as bacc
    from concourse import mybir as _mybir
    from concourse.bass_utils import run_bass_kernel_spmd as run

    x = {k.replace("L0_attn_", "").replace("L0_", ""): np.asarray(v) for k, v in inputs.items()}
    c = np.ascontiguousarray
    sel = np.zeros((2 * HEADS, PAIRS, 128), np.float32)
    for r in range(2 * HEADS):
        h = r % HEADS
        sel[r, h // 2, 64 * (h % 2):64 * (h % 2) + 64] = 1.0
    tie = np.zeros((128, EXPERTS, EXPERTS), np.float32)
    for e in range(EXPERTS):
        tie[:, e, :e] = 1.0
    chunks = lambda b, n: b.reshape(b.shape[0], n, 128).transpose(0, 2, 1)
    par = [x[k].reshape(LAYERS, D, 1) for k in ("ln1_g", "ln1_b", "ln2_g", "ln2_b", "b_ff2")]
    arrays = {
        "xT": c(x["x"].reshape(TOK, D).T),
        "ident": np.eye(128, dtype=np.float32),
        "rT": position_encoding(np),
        "sel": sel.reshape(2 * HEADS, PAIRS * 128),
        "tie": tie,
        "W_qkv": c(x["W_qkv"]), "W_r": c(x["W_r"]), "W_o": c(x["W_o"]),
        "W_ff1": c(x["W_ff1"]), "W_ff2": c(x["W_ff2"]),
        "u": c(x["u"].reshape(1, HEADS * DH)), "v": c(x["v"].reshape(1, HEADS * DH)),
        "par": c(np.concatenate(par + [chunks(x["b_ff1"], 4)], axis=2)),
        "w_routerT": c(x["ffn_w_router"].T),
        "w_upT": c(x["ffn_w_up"].transpose(0, 2, 1)),
        "w_downT": c(x["ffn_w_down"].transpose(0, 2, 1)),
        "bias_e": c(np.concatenate([chunks(x["ffn_b_up"], 4), x["ffn_b_down"].reshape(EXPERTS, D, 1)], axis=2)),
    }
    nc = bacc.Bacc("TRN2", target_bir_lowering=False, num_devices=1)
    args = {k: nc.dram_tensor("in_" + k, v.shape, _mybir.dt.from_np(v.dtype), kind="ExternalInput").ap()
            for k, v in arrays.items()}
    out = nc.dram_tensor("out_T", (D, TOK), _mybir.dt.float32, kind="ExternalOutput").ap()
    build(nc, args, out)
    r = run(nc, [{"in_" + k: v for k, v in arrays.items()}], core_ids=[0])
    return c(r.results[0]["out_T"].T).reshape(BATCH, SEQ, D)
```

```python
from contextlib import ExitStack

import concourse.bass as bass
from concourse import mybir

LAYERS, BATCH, SEQ, D, HEADS, DH, FF = 4, 2, 1024, 128, 16, 64, 512
EXPERTS, UP = 8, 512
PAIRS = HEADS // 2
KT = SEQ // 128
HALF = 512
TOK = BATCH * SEQ
MX_TILES = 32
PROJ = [("k", 0), ("k", 1), ("q", 0), ("q", 1)]
PROJ_AT = {6: 0, 8: 1, 11: 2, 13: 3}
MX_AT = [0, 0, 0, 2, 3, 2, 3, 2, 3, 2, 3, 2, 3, 2, 3, 2]
SPLIT_AT = 4
EXP0 = 64
TAIL_AT = 1
SUM_AT = 9


def build(nc, a, out_t):
    f32 = mybir.dt.float32
    f32r = mybir.dt.float32r
    ALU = mybir.AluOpType
    ACT = mybir.ActivationFunctionType
    AX = mybir.AxisListType.X
    SCALE = DH ** -0.5
    EPS = 1e-5

    ctx = ExitStack()
    with ctx:
        def sb(name, shape, dt=f32):
            return ctx.enter_context(nc.sbuf_tensor(name, shape, dt))

        def sem(name):
            return ctx.enter_context(nc.semaphore(name))

        xn_dram = nc.dram_tensor("xn_scratch", [BATCH, D, SEQ], f32).ap()
        g_dram = nc.dram_tensor("gate_scratch", [BATCH, D, SEQ], f32).ap()
        route_dram = nc.dram_tensor("route_scratch", [EXPERTS, TOK], f32).ap()
        v_dram = nc.dram_tensor("v_scratch", [KT, 128, HEADS * DH], f32).ap()
        c_dram = nc.dram_tensor("c_scratch", [HEADS, 2, SEQ], f32).ap()
        rowsum_dram = nc.dram_tensor("rowsum_scratch", [PAIRS, 2, SEQ], f32).ap()

        ident = sb("ident", [128, 128])
        r_hi = sb("r_hi", [D, SEQ], f32r)
        r_lo = sb("r_lo", [D, SEQ], f32r)
        sel = sb("sel", [2 * HEADS, PAIRS, 128], f32r)
        ones = sb("ones", [128, 64])
        zeros = sb("zeros", [128, HALF])
        hT = sb("hT", [D, SEQ])
        h_hi = sb("h_hi", [D, SEQ], f32r)
        h_lo = sb("h_lo", [D, SEQ], f32r)
        big = sb("big", [128, 8 * SEQ])
        probs = sb("probs", [128, 4, HALF])
        acc = sb("acc", [128, 2, 2, HALF])
        w_o = sb("w_o", [128, PAIRS, D])
        w_f1 = sb("w_f1", [D, FF])
        w_f2 = sb("w_f2", [128, 4, D])
        par = sb("par", [D, 9])
        q1 = sb("q1", [128, 2, 2, SEQ], f32r)
        q2 = sb("q2", [128, 2, 2, SEQ], f32r)
        k1 = sb("k1", [128, 2, 2, SEQ], f32r)
        k2 = sb("k2", [128, 2, 2, SEQ], f32r)
        qm = sb("qm", [128, 2, SEQ], f32r)
        kq_hi = sb("kq_hi", [128, 2, SEQ], f32r)
        kq_lo = sb("kq_lo", [128, 2, SEQ], f32r)
        v_slot = sb("v_slot", [128, 2, KT, 128])
        w_raw = sb("w_raw", [D, 3, 128])
        w_hi = sb("w_hi", [D, 3, 128], f32r)
        w_lo = sb("w_lo", [D, 3, 128], f32r)
        mx = sb("mx", [128, 2, 2, 4, 2])
        mx_all = sb("mx_all", [128, 2, 2, 4])
        m_hl = sb("m_hl", [128, 2, 2, 2, 4], f32r)
        srow = sb("srow", [128, SEQ])
        rc = sb("rc", [128, 128])
        rc_hi = sb("rc_hi", [128, 128], f32r)
        rc_lo = sb("rc_lo", [128, 128], f32r)
        rrow = sb("rrow", [2 * HEADS, SEQ], f32r)
        bst = sb("bst", [128, 4, 6])
        mv = sb("mv", [128, 4, 2])
        var4 = sb("var4", [128, 4])
        rs_l = sb("rs_l", [128, 4])
        rs_y = sb("rs_y", [128, 4])
        rs_t = sb("rs_t", [128, 3, 4])
        rstd = sb("rstd", [128, 4])
        c_hl = sb("c_hl", [HEADS, 2, SEQ], f32r)
        wku = sb("wku", [D, HEADS])
        wrv = sb("wrv", [D, HEADS])
        bias_e = sb("bias_e", [128, 2, 5])
        lg = sb("lg", [128, 16, EXPERTS])
        w_rt = sb("w_rt", [D, EXPERTS])
        tie = sb("tie", [128, EXPERTS, EXPERTS])
        rt1 = sb("rt1", [128, 16, EXPERTS])
        rt2 = sb("rt2", [128, 16, EXPERTS])
        rt3 = sb("rt3", [128, 16])

        vecT = big[:, :].rearrange("p (a n) -> p a n", a=PAIRS)
        st_wv, st_rT, st_t0, st_t1, st_wk, st_wr, st_u, st_v = (big[:, SEQ * i:SEQ * (i + 1)] for i in range(8))
        hid = big[:, 0:4 * SEQ].rearrange("p (f n) -> p f n", f=4)
        flat_acc = acc[:, :, :, :].rearrange("p a b n -> p (a b n)")
        flat_probs = probs[:, :, :].rearrange("p a n -> p (a n)")
        xT = flat_acc[:, 0:SEQ]
        yT = flat_probs[:, 0:SEQ].rearrange("p (t n) -> p t n", n=128)
        xn = big[:, 0:TOK]
        gacc = big[:, TOK:2 * TOK]
        gate_b = [big[:, TOK * (2 + i):TOK * (3 + i)] for i in range(2)]
        e_up = [w_f1[:, :], w_f2[:, :, :].rearrange("p a n -> p (a n)")]
        e_dn = [w_o[:, 0:4, :], w_o[:, 4:8, :]]
        e_h = [probs, acc[:, :, :, :].rearrange("p a b n -> p (a b) n")]
        e_tmp = v_slot[:, 0, 0:4, :].rearrange("p a n -> p (a n)")
        route_t = v_slot[0:EXPERTS, :, :, :].rearrange("p a b n -> p (a b n)")
        cmp_a = gate_b[0][:, 0:1024].rearrange("p (t e j) -> p t e j", t=16, e=EXPERTS)
        cmp_b = gate_b[0][:, 1024:2048].rearrange("p (t e j) -> p t e j", t=16, e=EXPERTS)
        sel_raw = gate_b[1][0:2 * HEADS, 0:1024]

        bank = [ctx.enter_context(nc.psum_tensor(f"bank{i}", [128, HALF], f32)) for i in range(4)]
        mxp = ctx.enter_context(nc.psum_tensor("mxp", [128, 2, HALF], f32))
        pv = ctx.enter_context(nc.psum_tensor("pv", [128, HALF], f32))
        pj = ctx.enter_context(nc.psum_tensor("pj", [128, HALF], f32))
        acc_bank = [pv, pj]

        consts = sem("consts_loaded")
        ready0 = sem("constants_ready")
        seeded = sem("semaphores_seeded")
        x_in = sem("x_loaded")
        ln_t, ln_var, ln_rs, ln_y, ln_b, ln_out = (sem(s) for s in (
            "ln_transposed", "ln_variance", "ln_rstd", "ln_normalised", "ln_back", "ln_out"))
        dve_chain, act_chain = sem("dve_chain"), sem("act_chain")
        xn_out = sem("xn_stored")
        lg_done, route_ln, route_ex, route_g, route_tr, route_cp, route_out = (sem(s) for s in (
            "logits", "route_sub", "route_exp", "route_gates", "route_transposed", "route_copied", "route_stored"))
        e_in = [sem("expert_loaded0"), sem("expert_loaded1")]
        up_done, gelu_done, down_done, mo_acc = (sem(s) for s in ("up_done", "gelu_done", "down_done", "expert_added"))
        sig, gfin, g_out = sem("sigmoid_done"), sem("gate_final"), sem("gate_stored")
        h_in = sem("h_loaded")
        cw_in, layer_in, weights_in = sem("c_weights_loaded"), sem("stage_a_loaded"), sem("layer_weights_loaded")
        hh_done, hl_done = sem("h_hi_done"), sem("h_lo_done")
        wc_done, wc_chain = sem("c_weights_done"), sem("c_weights_chain")
        c_mm, c_hi_done, c_lo_done, c_out = sem("c_mm"), sem("c_hi_done"), sem("c_lo_done"), sem("c_stored")
        v_mm, v_ev, v_out = sem("v_mm"), sem("v_evacuated"), [sem("v_stored0"), sem("v_stored1")]
        wraw_in, w_split, proj = sem("w_raw_loaded"), sem("w_split"), sem("projected")
        hi_done, lo_done = sem("proj_hi_done"), sem("proj_lo_done")
        k2_rows, qm_rows, score_tiles = sem("k2_written"), sem("qm_written"), sem("score_tiles_written")
        v_in = [sem("v_slot_loaded0"), sem("v_slot_loaded1")]
        m_chain, split_chain = sem("m_chain"), sem("w_hi_done")
        mx_mm, mx_red, m_split = sem("max_tile"), sem("max_reduced"), sem("max_split")
        m_row = [sem("m_rows0"), sem("m_rows1")]
        st_done, exp_done, pv_done = sem("scores"), sem("exps"), sem("pv_step")
        add_done = [sem("sum_added0"), sem("sum_added1")]
        pv_ev, sum_mm, sum_cp, sum_out = sem("pv_evacuated"), sem("sum_mm"), sem("sum_copied"), sem("sums_stored")
        rc_in, rc_chain, rc_done, rrow_in = sem("sums_loaded"), sem("rc_chain"), sem("rc_done"), sem("rc_rows")
        bc_mm, vec_norm, op_done, x1_done = sem("rc_broadcast"), sem("vec_normalised"), sem("out_projected"), sem("residual_done")
        f1_mm, f1_act, f2_mm, x2_done = sem("ff1_mm"), sem("ff1_act"), sem("ff2_mm"), sem("ff2_out")
        fin_in, fin_mul, fin_done, res_out = sem("final_loaded"), sem("final_mul"), sem("final_done"), sem("result_stored")
        SEEDS = [(exp_done, EXP0 + 4), (pv_done, 2), (add_done[0], 2), (add_done[1], 2), (sum_cp, 1), (pv_ev, 1),
                 (sum_mm, 3), (sum_out, 1), (k2_rows, 1), (qm_rows, 1), (score_tiles, 1), (mx_mm, 1), (mx_red, 2),
                 (st_done, 1), (op_done, 1),
                 (proj, 1), (w_split, 1), (m_row[0], 1), (m_row[1], 1),
                 (mo_acc, 8), (gelu_done, 4), (down_done, 2), (fin_done, 2), (res_out, 16)]

        block = ctx.enter_context(nc.Block())

        @block.sync
        def _(sp):
            for s, k in SEEDS:
                sp.sem_inc(s, k)
            sp.sem_inc(seeded, 1)
            sp.dma_start(xT, a["xT"][:, 0:SEQ]).then_inc(x_in, 16)
            sp.dma_start(ident[:, :], a["ident"]).then_inc(consts, 16)
            sp.dma_start(w_rt[:, :], a["w_routerT"]).then_inc(consts, 16)
            sp.dma_start(tie[:, :, :], a["tie"]).then_inc(consts, 16)
            sp.dma_start(st_rT, a["rT"]).then_inc(consts, 16)
            sp.dma_start(sel_raw, a["sel"]).then_inc(consts, 16)
            sp.wait_ge(ln_t, 2)
            sp.dma_start(xT, a["xT"][:, SEQ:TOK]).then_inc(x_in, 16)
            for b in range(BATCH):
                sp.wait_ge(ln_out, 2 * (b + 1))
                sp.dma_start(xn_dram[b], xn[:, b * SEQ:(b + 1) * SEQ]).then_inc(xn_out, 16)
            sp.wait_ge(route_cp, 4)
            sp.dma_start(route_dram, route_t).then_inc(route_out, 16)
            sp.wait_ge(route_out, 16)
            sp.wait_ge(ready0, 3)
            with sp.Fori(0, EXPERTS // 2) as ep:
                for s in range(2):
                    e = ep * 2 + s
                    sp.wait_ge(mo_acc, e * 4 + 4)
                    sp.dma_start(e_up[s], a["w_upT"][e]).then_inc(e_in[s], 16)
                    sp.dma_start(e_dn[s], a["w_downT"][e].rearrange("(c p) d -> p c d", p=128)).then_inc(e_in[s], 16)
                    sp.dma_start(bias_e[:, s, :], a["bias_e"][e]).then_inc(e_in[s], 16)
                    sp.dma_start(gate_b[s], route_dram[bass.ds(e, 1), :].broadcast_to([128, TOK])).then_inc(e_in[s], 16)
            sp.wait_ge(gfin, 1)
            for b in range(BATCH):
                sp.dma_start(g_dram[b], gacc[:, b * SEQ:(b + 1) * SEQ]).then_inc(g_out, 16)
            sp.wait_ge(g_out, 16 * BATCH)
            sp.wait_ge(xn_out, 16 * BATCH)

            def load_w(m, l, p):
                sp.wait_ge(w_split, m + 1)
                sp.wait_ge(seeded, 1)
                sp.dma_start(w_raw[:, 0:2, :], a["W_qkv"][l, :, 0:2 * SEQ].rearrange(
                    "d (t a n) -> d t a n", t=2, n=128)[:, :, p, :]).then_inc(wraw_in, 16)
                sp.dma_start(w_raw[:, 2, :], a["W_r"][l].rearrange("d (a n) -> d a n", n=128)[:, p, :]).then_inc(wraw_in, 16)

            def raw(x):
                return x.bitcast(f32)

            def k2_tile(m, s, c_rows):
                sp.wait_ge(lo_done, 4 * m + 2)
                for h in range(2):
                    sp.dma_start(raw(k2[0:64, s, h, :]), raw(kq_hi[64 * h:64 * h + 64, 0, :])).then_inc(k2_rows, 16)
                    c_rows(h)

            def qm_tile(m):
                sp.wait_ge(lo_done, 4 * m + 4)
                sp.wait_ge(mx_mm, 32 * m + 1)
                for h in range(2):
                    sp.dma_start(raw(qm[0:64, h, :]), raw(kq_hi[64 * h:64 * h + 64, 1, :])).then_inc(qm_rows, 16)

            def rest_tiles(s):
                for h in range(2):
                    hs = slice(64 * h, 64 * h + 64)
                    sp.dma_start(raw(k1[0:64, s, h, :]), raw(kq_hi[hs, 0, :])).then_inc(score_tiles, 16)
                    sp.dma_start(raw(k1[64:128, s, h, :]), raw(kq_lo[hs, 0, :])).then_inc(score_tiles, 16)
                    sp.dma_start(raw(q1[0:64, s, h, :]), raw(kq_hi[hs, 1, :])).then_inc(score_tiles, 16)
                    sp.dma_start(raw(q1[64:128, s, h, :]), raw(kq_hi[hs, 1, :])).then_inc(score_tiles, 16)
                    sp.dma_start(raw(q2[0:64, s, h, :]), raw(kq_lo[hs, 1, :])).then_inc(score_tiles, 16)

            def load_v(g, m, p, s):
                sp.dma_start(v_slot[:, s, :, :], v_dram.rearrange(
                    "t k (a n) -> k t a n", n=128)[:, :, p, :]).then_inc(v_in[s], 16)

            def m_rows(m, s, half):
                sp.wait_ge(m_split, 2 * m + half + 1)
                for h in range(2):
                    for i in range(2):
                        sp.dma_start(raw(q2[66 + i:67 + i, s, h, half * HALF:(half + 1) * HALF]),
                                     raw(m_hl[:, half, h, i, :])).then_inc(m_row[half], 16)

            def store_sums(n, p):
                sp.wait_ge(sum_cp, 2 * n + 3)
                sp.wait_ge(seeded, 1)
                for h in range(2):
                    sp.dma_start(rowsum_dram.rearrange("a h n -> h a n")[h, p, :], srow[64 * h:64 * h + 1, :]).then_inc(sum_out, 16)

            def unit(g, l, p, s, prev=True, proj2=True, nxt=True):
                n = g * PAIRS + p
                if nxt:
                    qm_tile(n + 1)
                if proj2:
                    load_w(n + 2, l, p + 2)
                if nxt:
                    sp.wait_ge(pv_done, 16 * n + 2)
                    rest_tiles(1 - s)
                    load_v(g, n + 1, p + 1, 1 - s)
                if prev:
                    store_sums(n - 1, p - 1)
                if nxt:
                    m_rows(n + 1, 1 - s, 0)
                if proj2:
                    sp.wait_ge(st_done, 32 * n + 33)
                    k2_tile(n + 2, s, c_from_dram(p + 2, s))
                if nxt:
                    m_rows(n + 1, 1 - s, 1)

            def c_from_dram(p, s):
                return lambda h: sp.dma_start(raw(k2[64:66, s, h, :]), c_dram[2 * p + h]).then_inc(k2_rows, 16)

            with sp.Fori(0, BATCH) as b:
                sp.wait_ge(res_out, 16 * b + 16)
                sp.wait_ge(fin_done, 2 * b + 2)
                sp.dma_start(hT[:, :], xn_dram[b]).then_inc(h_in, 16)
                with sp.Fori(0, LAYERS) as l:
                    g = b * LAYERS + l
                    load_w(g * PAIRS, l, 0)
                    sp.wait_ge(op_done, 2 * g + 1)
                    sp.dma_start(st_wk, a["W_qkv"][l, :, SEQ:2 * SEQ]).then_inc(cw_in, 16)
                    sp.dma_start(st_u, a["u"].broadcast_to([128, SEQ])).then_inc(cw_in, 16)
                    sp.dma_start(st_wr, a["W_r"][l]).then_inc(cw_in, 16)
                    sp.dma_start(st_v, a["v"].broadcast_to([128, SEQ])).then_inc(cw_in, 16)
                    sp.wait_ge(ln_out, 4 * g + 4)
                    sp.wait_ge(seeded, 1)
                    sp.dma_start(st_rT, a["rT"]).then_inc(layer_in, 16)
                    sp.dma_start(st_wv, a["W_qkv"][l, :, 2 * SEQ:3 * SEQ]).then_inc(layer_in, 16)
                    load_w(g * PAIRS + 1, l, 1)
                    sp.dma_start(w_o[:, :, :], a["W_o"][l].rearrange("(a p) d -> p a d", p=128)).then_inc(weights_in, 16)
                    sp.dma_start(w_f1[:, :], a["W_ff1"][l]).then_inc(weights_in, 16)
                    sp.dma_start(w_f2[:, :, :], a["W_ff2"][l].rearrange("(c p) d -> p c d", p=128)).then_inc(weights_in, 16)
                    sp.dma_start(par[:, :], a["par"][l]).then_inc(weights_in, 16)
                    sp.wait_ge(c_lo_done, 2 * g + 2)
                    sp.wait_ge(c_hi_done, 2 * g + 2)

                    def first_c(h):
                        sp.dma_start(raw(k2[64:66, 0, h, :]), raw(c_hl[h:h + 1, :, :])).then_inc(k2_rows, 16)

                    k2_tile(g * PAIRS, 0, first_c)
                    qm_tile(g * PAIRS)
                    rest_tiles(0)
                    sp.dma_start(c_dram[:, 0, :], raw(c_hl[:, 0, :])).then_inc(c_out, 16)
                    sp.dma_start(c_dram[:, 1, :], raw(c_hl[:, 1, :])).then_inc(c_out, 16)
                    sp.wait_ge(c_out, 32 * g + 32)
                    m_rows(g * PAIRS, 0, 0)
                    for i in range(2):
                        sp.wait_ge(v_out[i], 64 * g + 64)
                    load_v(g, g * PAIRS, 0, 0)
                    k2_tile(g * PAIRS + 1, 1, c_from_dram(1, 1))
                    m_rows(g * PAIRS, 0, 1)
                    with sp.Fori(0, 1) as p:
                        unit(g, l, p, 0, prev=False)
                    with sp.Fori(0, 2) as j:
                        unit(g, l, j * 2 + 1, 1)
                        unit(g, l, j * 2 + 2, 0)
                    with sp.Fori(5, 6) as p:
                        unit(g, l, p, 1)
                    with sp.Fori(6, 7) as p:
                        unit(g, l, p, 0, proj2=False)
                    with sp.Fori(7, 8) as p:
                        unit(g, l, p, 1, proj2=False, nxt=False)
                    store_sums(g * PAIRS + 7, 7)
                    sp.wait_ge(sum_out, 32 * PAIRS * (g + 1) + 1)
                    sp.dma_start(rc[:, :], rowsum_dram.rearrange("a h (c n) -> (a h c) n", n=128)).then_inc(rc_in, 16)
                    sp.wait_ge(rc_done, g + 1)
                    sp.dma_start(raw(rrow[0:HEADS, :]), raw(rc_hi[:, :])).then_inc(rrow_in, 16)
                    sp.dma_start(raw(rrow[HEADS:2 * HEADS, :]), raw(rc_lo[:, :])).then_inc(rrow_in, 16)
                sp.wait_ge(ln_out, 4 * b * LAYERS + 4 * LAYERS + 4)
                sp.dma_start(st_wv, a["xT"].rearrange("d (b n) -> d b n", b=BATCH)[:, b, :]).then_inc(fin_in, 16)
                sp.dma_start(st_wk, g_dram[b]).then_inc(fin_in, 16)
                sp.wait_ge(fin_done, 2 * b + 4)
                sp.dma_start(out_t.rearrange("d (b n) -> d b n", b=BATCH)[:, b, :], st_t0).then_inc(res_out, 16)
            sp.wait_ge(res_out, BATCH * 16 + 16)

        @block.tensor
        def _(pe):
            def ln(H, half):
                for i in range(4):
                    t = half * 4 + i
                    last = nc.tensor.transpose(mxp[:, half, i * 128:(i + 1) * 128], xT[:, t * 128:(t + 1) * 128], ident[:, :])
                last.then_inc(ln_t, 1)

            def ln_back(H, half):
                pe.wait_ge(ln_y, H + 1)
                for i in range(4):
                    last = nc.tensor.transpose(mxp[:, half, i * 128:(i + 1) * 128], yT[:, half * 4 + i, :], ident[:, :])
                last.then_inc(ln_b, 1)

            pe.wait_ge(seeded, 1)
            pe.wait_ge(consts, 80)
            for b in range(BATCH):
                pe.wait_ge(x_in, 16 * (b + 1))
                for half in range(2):
                    if b:
                        pe.wait_ge(ln_out, half + 1)
                    ln(2 * b + half, half)
                for half in range(2):
                    ln_back(2 * b + half, half)
            pe.wait_ge(ln_out, 4)
            for t in range(16):
                last = nc.tensor.matmul(mxp[:, 0, t * EXPERTS:(t + 1) * EXPERTS], xn[:, t * 128:(t + 1) * 128],
                                        w_rt[:, :], start=True, stop=True)
            last.then_inc(lg_done, 1)
            pe.wait_ge(route_g, 1)
            for t in range(16):
                last = nc.tensor.transpose(bank[t // 4][0:EXPERTS, (t % 4) * 128:(t % 4 + 1) * 128], lg[:, t, :], ident[:, :])
                if t % 4 == 3:
                    last.then_inc(route_tr, 1)
            pe.wait_ge(route_cp, 4)

            with pe.Fori(0, EXPERTS // 2) as ep:
                for s in range(2):
                    e = ep * 2 + s

                    def up(tc):
                        for f in range(4):
                            pe.wait_ge(gelu_done, (e * 4 + tc) * 4 + f + 1)
                            nc.tensor.matmul(bank[f][:, :], e_up[s][:, f * 128:(f + 1) * 128],
                                             xn[:, tc * HALF:(tc + 1) * HALF], start=True, stop=True).then_inc(up_done, 1)

                    def down(tc):
                        pe.wait_ge(mo_acc, e * 4 + tc + 7)
                        pe.wait_ge(gelu_done, (e * 4 + tc) * 4 + 8)
                        for f in range(4):
                            last = nc.tensor.matmul(acc_bank[tc % 2][:, :], e_dn[s][:, f, :], e_h[tc % 2][:, f, :],
                                                    start=(f == 0), stop=(f == 3))
                        last.then_inc(down_done, 1)

                    pe.wait_ge(e_in[s], ep * 64 + 64)
                    up(0)
                    for tc in range(4):
                        if tc < 3:
                            up(tc + 1)
                        down(tc)

            def project(m, i, after=(1, 2, 3)):
                kind, c = PROJ[i]
                if i in after:
                    pe.wait_ge(lo_done, 4 * m + i)
                cols = slice(c * HALF, (c + 1) * HALF)
                w = 1 if kind == "k" else 0
                ops = [(w_hi, w, h_hi), (w_hi, w, h_lo), (w_lo, w, h_hi)]
                if kind == "k":
                    ops += [(w_hi, 2, r_hi), (w_hi, 2, r_lo), (w_lo, 2, r_hi)]
                for j, (wt, k, x) in enumerate(ops):
                    last = nc.tensor.matmul(pj[:, :], wt[:, k, :], x[:, cols], start=(j == 0), stop=(j == len(ops) - 1))
                last.then_inc(proj, 1)

            def max_tile(m, s, t):
                if t == 0:
                    pe.wait_ge(k2_rows, 64 * m + 65)
                    pe.wait_ge(qm_rows, 32 * m + 33)
                half, h, j, c = t // 16, t // 8 % 2, t // 2 % 4, t % 2
                pe.wait_ge(mx_red, 32 * m + t + 1)
                w = qm[0:66, h, half * HALF:(half + 1) * HALF].rearrange("p (q j) -> p j q", j=4)[:, j, :]
                nc.tensor.matmul(mxp[:, c, :], w, k2[0:66, s, h, c * HALF:(c + 1) * HALF],
                                 start=True, stop=True).then_inc(mx_mm, 1)

            def scores(n, s, i):
                half, kt, h = i // 16, i // 2 % 8, i % 2
                if i % 16 == 0:
                    pe.wait_ge(m_row[half], 64 * n + 65)
                    pe.wait_ge(score_tiles, 160 * n + 161)
                pe.wait_ge(exp_done, EXP0 + 32 * n + i + 1)
                ks, qs = slice(kt * 128, (kt + 1) * 128), slice(half * HALF, (half + 1) * HALF)
                nc.tensor.matmul(bank[i % 4][:, :], k1[:, s, h, ks], q1[:, s, h, qs], start=True, stop=False)
                nc.tensor.matmul(bank[i % 4][:, :], k2[0:68, s, h, ks], q2[0:68, s, h, qs],
                                 start=False, stop=True).then_inc(st_done, 1)

            def sums(n, half):
                for h in range(2):
                    pe.wait_ge(add_done[h], 16 * n + 8 * half + 10)
                    last = nc.tensor.matmul(pj[64 * h:64 * h + 64, :], ones[:, :], acc[:, half, h, :], start=True, stop=True)
                last.then_inc(sum_mm, 1)

            def unit(g, p, s, prev=True, proj2=True, nxt=True):
                n = g * PAIRS + p
                t = 0
                for step in range(16):
                    half, kt = step // 8, step % 8
                    tiles = MX_AT[step] if nxt else 0
                    if proj2 and step in PROJ_AT:
                        i = PROJ_AT[step]
                        if i == 0:
                            pe.wait_ge(w_split, n + 4)
                            pe.wait_ge(sum_cp, 2 * n + 1)
                        if i == 2:
                            pe.wait_ge(sum_cp, 2 * n + 2)
                        project(n + 2, i, after=(1, 3))
                    if tiles > 0:
                        max_tile(n + 1, 1 - s, t)
                        t += 1
                    if step < 15:
                        scores(n, s, 2 * step + 2)
                        scores(n, s, 2 * step + 3)
                    elif nxt:
                        scores(n + 1, 1 - s, 0)
                        scores(n + 1, 1 - s, 1)
                    if tiles > 1:
                        max_tile(n + 1, 1 - s, t)
                        t += 1
                    if kt == 0:
                        pe.wait_ge(pv_ev, 2 * n + half + 1)
                    if step == 0:
                        pe.wait_ge(v_in[s], 8 * n - 8 * s + 16)
                    for h in range(2):
                        i = 2 * step + h
                        pe.wait_ge(exp_done, EXP0 + 32 * n + i + 5)
                        last = nc.tensor.matmul(pv[64 * h:64 * h + 64, :], v_slot[:, s, kt, 64 * h:64 * h + 64],
                                                probs[:, i % 4, :], start=(kt == 0), stop=(kt == 7))
                    last.then_inc(pv_done, 1)
                    if tiles > 2:
                        max_tile(n + 1, 1 - s, t)
                        t += 1
                    if prev and step == TAIL_AT:
                        if nxt:
                            pe.wait_ge(lo_done, 4 * n + 8)
                        pe.wait_ge(sum_cp, 2 * n)
                        sums(n - 1, 1)
                    if step == SUM_AT:
                        if proj2:
                            pe.wait_ge(lo_done, 4 * n + 10)
                        pe.wait_ge(sum_cp, 2 * n + 1)
                        sums(n, 0)

            with pe.Fori(0, BATCH) as b:
                with pe.Fori(0, LAYERS) as l:
                    g = b * LAYERS + l
                    n0 = g * PAIRS
                    pe.wait_ge(ln_out, 4 * g + 4)
                    pe.wait_ge(w_split, n0 + 2)
                    for i in range(4):
                        if i < 2:
                            pe.wait_ge(hh_done, 2 * g + i + 1)
                            pe.wait_ge(hl_done, 2 * g + i + 1)
                        project(n0, i)
                    pe.wait_ge(layer_in, 32 * g + 32)
                    pe.wait_ge(wc_done, g + 1)
                    for half in range(2):
                        hs = slice(half * HALF, (half + 1) * HALF)
                        nc.tensor.matmul(bank[half][0:HEADS, :], wku[:, :], hT[:, hs], start=True, stop=False)
                        nc.tensor.matmul(bank[half][0:HEADS, :], wrv[:, :], st_rT[:, hs], start=False, stop=True)\
                            .then_inc(c_mm, 1)
                    t = 0
                    for i in range(16):
                        if i >= 4:
                            pe.wait_ge(v_ev, 16 * g + i - 3)
                        b_i = (i + 2) % 4
                        if i in (2, 3):
                            pe.wait_ge(c_lo_done, 2 * g + i - 1)
                        nc.tensor.matmul(bank[b_i][:, :], hT[:, (i // 2) * 128:(i // 2 + 1) * 128],
                                         st_wv[:, (i % 2) * HALF:(i % 2 + 1) * HALF], start=True, stop=True).then_inc(v_mm, 1)
                        if i >= 7:
                            for _ in range(2):
                                max_tile(n0, 0, t)
                                t += 1
                    pe.wait_ge(w_split, n0 + 3)
                    for i in range(4):
                        pe.wait_ge(lo_done, 4 * (n0 + 1) + i)
                        project(n0 + 1, i, after=())
                        if t < MX_TILES:
                            max_tile(n0, 0, t)
                            t += 1
                    while t < MX_TILES:
                        max_tile(n0, 0, t)
                        t += 1
                    pe.wait_ge(v_ev, 16 * g + 16)
                    scores(n0, 0, 0)
                    scores(n0, 0, 1)
                    with pe.Fori(0, 1) as p:
                        unit(g, p, 0, prev=False)
                    with pe.Fori(0, 2) as j:
                        unit(g, j * 2 + 1, 1)
                        unit(g, j * 2 + 2, 0)
                    with pe.Fori(5, 6) as p:
                        unit(g, p, 1)
                    with pe.Fori(6, 7) as p:
                        unit(g, p, 0, proj2=False)
                    with pe.Fori(7, 8) as p:
                        unit(g, p, 1, proj2=False, nxt=False)
                    pe.wait_ge(sum_cp, 2 * (n0 + 7) + 2)
                    sums(n0 + 7, 1)
                    pe.wait_ge(rrow_in, 32 * g + 32)
                    pe.wait_ge(weights_in, 64 * g + 64)
                    pe.wait_ge(exp_done, EXP0 + 32 * (n0 + PAIRS) + 4)
                    pe.wait_ge(sum_cp, 2 * (n0 + PAIRS) + 1)
                    pe.wait_ge(pv_ev, 2 * (n0 + PAIRS) + 1)
                    for i in range(2 * PAIRS + 3):
                        if i < 2 * PAIRS:
                            if i >= 4:
                                pe.wait_ge(vec_norm, 2 * PAIRS * g + i - 3)
                            nc.tensor.matmul(bank[i % 4][:, :], sel[:, i // 2, :], rrow[:, (i % 2) * HALF:(i % 2 + 1) * HALF],
                                             start=True, stop=True).then_inc(bc_mm, 1)
                        if i >= 3:
                            o = i - 3
                            pe.wait_ge(vec_norm, 2 * PAIRS * g + o + 1)
                            last = nc.tensor.matmul(acc_bank[o % 2][:, :], w_o[:, o // 2, :],
                                                    vecT[:, o // 2, (o % 2) * HALF:(o % 2 + 1) * HALF],
                                                    start=(o < 2), stop=(o >= 2 * PAIRS - 2))
                            if o >= 2 * PAIRS - 2:
                                last.then_inc(op_done, 1)
                    H = 4 * g + 4
                    for half in range(2):
                        pe.wait_ge(x1_done, 2 * g + half + 1)
                        ln(H + half, half)
                    for half in range(2):
                        ln_back(H + half, half)
                        pe.wait_ge(ln_out, H + half + 1)
                        hs = slice(half * HALF, (half + 1) * HALF)
                        for f in range(4):
                            if half:
                                pe.wait_ge(f1_act, 8 * g + f + 1)
                            nc.tensor.matmul(bank[f][:, :], w_f1[:, f * 128:(f + 1) * 128], hT[:, hs], start=True, stop=True)\
                                .then_inc(f1_mm, 1)
                    for half in range(2):
                        pe.wait_ge(f1_act, 8 * g + 4 * half + 4)
                        hs = slice(half * HALF, (half + 1) * HALF)
                        for f in range(4):
                            last = nc.tensor.matmul(acc_bank[half][:, :], w_f2[:, f, :], hid[:, f, hs], start=(f == 0), stop=(f == 3))
                        last.then_inc(f2_mm, 1)
                    for half in range(2):
                        pe.wait_ge(x2_done, 2 * g + half + 1)
                        ln(H + 2 + half, half)
                    for half in range(2):
                        ln_back(H + 2 + half, half)

        @block.scalar
        def _(act):
            def ln(H, half, out, scale=1.0, bias=0.0):
                act.wait_ge(ln_var, H + 1)
                nc.scalar.activation(rs_l[:, :], var4[:, :], ACT.Ln).then_inc(act_chain, 1)
                act.wait_ge(act_chain, H + 1)
                nc.scalar.activation(rs_y[:, :], rs_l[:, :], ACT.Exp, scale=-0.5).then_inc(ln_rs, 1)

            def ln_finish(H, half, out, scale=1.0, bias=0.0):
                act.wait_ge(ln_b, H + 1)
                nc.scalar.activation(out, mxp[:, half, :], ACT.Identity, scale=scale, bias=bias).then_inc(ln_out, 1)

            act.wait_ge(seeded, 1)
            act.wait_ge(consts, 80)
            nc.scalar.activation(r_hi[:, :], st_rT, ACT.Copy).then_inc(ready0, 1)
            for b in range(BATCH):
                for half in range(2):
                    ln(2 * b + half, half, None)
                for half in range(2):
                    ln_finish(2 * b + half, half, xn[:, b * SEQ + half * HALF:b * SEQ + (half + 1) * HALF])
            act.wait_ge(route_ln, 1)
            nc.scalar.activation(rt1[:, :, :], rt1[:, :, :], ACT.Exp).then_inc(route_ex, 1)
            for i in range(4):
                act.wait_ge(route_tr, i + 1)
                nc.scalar.activation(route_t[:, i * HALF:(i + 1) * HALF], bank[i][0:EXPERTS, :], ACT.Copy).then_inc(route_cp, 1)
            with act.Fori(0, EXPERTS // 2) as ep:
                for s in range(2):
                    e = ep * 2 + s
                    act.wait_ge(e_in[s], ep * 64 + 64)
                    for tc in range(4):
                        act.wait_ge(down_done, e * 4 + tc + 1)
                        for f in range(4):
                            act.wait_ge(up_done, (e * 4 + tc) * 4 + f + 1)
                            nc.scalar.activation(e_h[tc % 2][:, f, :], bank[f][:, :], ACT.Gelu,
                                                 bias=bias_e[:, s, f:f + 1]).then_inc(gelu_done, 1)
            act.wait_ge(mo_acc, 4 * EXPERTS + 8)
            nc.scalar.activation(gate_b[0], gacc, ACT.Sigmoid).then_inc(sig, 1)

            def hi_half(m, i):
                kq, c = i // 2, i % 2
                if i == 0:
                    act.wait_ge(k2_rows, 64 * m + 1)
                    act.wait_ge(qm_rows, 32 * m + 1)
                    act.wait_ge(score_tiles, 160 * m + 1)
                act.wait_ge(proj, 4 * m + i + 2)
                nc.scalar.activation(kq_hi[:, kq, c * HALF:(c + 1) * HALF], pj[:, :], ACT.Copy).then_inc(hi_done, 1)

            def unit(g, p, prev=True, proj2=True):
                n = g * PAIRS + p
                for step in range(16):
                    act.wait_ge(pv_done, 16 * n + step + 1)
                    for h in range(2):
                        act.wait_ge(add_done[h], 16 * n + step + 1)
                        i = 2 * step + h
                        act.wait_ge(st_done, 32 * n + i + 2)
                        nc.scalar.activation(probs[:, i % 4, :], bank[i % 4][:, :], ACT.Exp, scale=SCALE).then_inc(exp_done, 1)
                    if prev and step == 0:
                        evacuate(n - 1, p - 1, 1)
                    if step == 8:
                        evacuate(n, p, 0)
                    if proj2 and step in PROJ_AT:
                        hi_half(n + 2, PROJ_AT[step])
                    if prev and step == TAIL_AT + 1:
                        sum_copy(n - 1, 1)
                    if step == SUM_AT + 1:
                        sum_copy(n, 0)

            def evacuate(n, p, half):
                act.wait_ge(pv_done, 16 * n + 8 * half + 10)
                nc.scalar.activation(big[:, bass.ds(p * SEQ + half * HALF, HALF)], pv[:, :], ACT.Copy).then_inc(pv_ev, 1)

            def sum_copy(n, half):
                act.wait_ge(sum_mm, 2 * n + half + 4)
                if half == 0:
                    act.wait_ge(sum_out, 32 * n + 1)
                nc.scalar.activation(srow[:, half * HALF:(half + 1) * HALF], pj[:, :], ACT.Copy).then_inc(sum_cp, 1)

            with act.Fori(0, BATCH) as b:
                with act.Fori(0, LAYERS) as l:
                    g = b * LAYERS + l
                    n0 = g * PAIRS
                    act.wait_ge(h_in, b * 16 + 16)
                    act.wait_ge(ln_out, 4 * g + 4)
                    for half in range(2):
                        hs = slice(half * HALF, (half + 1) * HALF)
                        nc.scalar.activation(h_hi[:, hs], hT[:, hs], ACT.Copy).then_inc(hh_done, 1)
                    for i in range(4):
                        hi_half(n0, i)
                    for half in range(2):
                        act.wait_ge(c_mm, 2 * g + half + 1)
                        nc.scalar.activation(c_hl[:, 0, half * HALF:(half + 1) * HALF], bank[half][0:HEADS, :], ACT.Copy)\
                            .then_inc(c_hi_done, 1)
                    for i in range(16):
                        t, c = i // 2, i % 2
                        act.wait_ge(v_mm, 16 * g + i + 1)
                        if i >= 4 and c == 0:
                            act.wait_ge(v_out[t % 2], 64 * g + 16 * (t // 2))
                        nc.scalar.activation((st_t0, st_t1)[t % 2][:, c * HALF:(c + 1) * HALF], bank[(i + 2) % 4][:, :],
                                             ACT.Copy).then_inc(v_ev, 1)
                        if c:
                            act.wait_ge(v_ev, 16 * g + i + 1)
                            act.dma_start(v_dram[t], (st_t0, st_t1)[t % 2]).then_inc(v_out[t % 2], 16)
                    for i in range(4):
                        hi_half(n0 + 1, i)
                    with act.Fori(0, 1) as p:
                        unit(g, p, prev=False)
                    with act.Fori(0, 4) as j:
                        unit(g, j + 1)
                    with act.Fori(5, 6) as p:
                        unit(g, p)
                    with act.Fori(6, 7) as p:
                        unit(g, p, proj2=False)
                    with act.Fori(7, 8) as p:
                        unit(g, p, proj2=False)
                    evacuate(n0 + 7, 7, 1)
                    sum_copy(n0 + 7, 1)
                    H = 4 * g + 4
                    act.wait_ge(weights_in, 64 * g + 64)
                    for half in range(2):
                        ln(H + half, half, None)
                    for half in range(2):
                        hs = slice(half * HALF, (half + 1) * HALF)
                        ln_finish(H + half, half, hT[:, hs], par[:, 0:1], par[:, 1:2])
                        for f in range(4):
                            act.wait_ge(f1_mm, 8 * g + 4 * half + f + 1)
                            nc.scalar.activation(hid[:, f, hs], bank[f][:, :], ACT.Relu, bias=par[:, 5 + f:6 + f])\
                                .then_inc(f1_act, 1)
                    for half in range(2):
                        hs = slice(half * HALF, (half + 1) * HALF)
                        act.wait_ge(f2_mm, 2 * g + half + 1)
                        nc.scalar.activation(xT[:, hs], acc_bank[half][:, :], ACT.Identity, bias=par[:, 4:5]).then_inc(x2_done, 1)
                    for half in range(2):
                        ln(H + 2 + half, half, None)
                    for half in range(2):
                        hs = slice(half * HALF, (half + 1) * HALF)
                        ln_finish(H + 2 + half, half, hT[:, hs], par[:, 2:3], par[:, 3:4])

        @block.vector
        def _(dve):
            def ln(H, half, chain):
                def link(ins, k):
                    ins.then_inc(dve_chain, 1)
                    dve.wait_ge(dve_chain, H * 6 + k)
                dve.wait_ge(ln_t, H + 1)
                for i in range(4):
                    last = nc.vector.bn_stats(bst[:, i, :], mxp[:, half, i * 128:(i + 1) * 128])
                link(last, 1)
                nc.vector.memset(rs_t[:, 2, :], 0.0)
                for i in range(4):
                    last = nc.vector.bn_aggr(mv[:, i, :], bst[:, i, :])
                link(last, 2)
                nc.vector.tensor_scalar(var4[:, :], mv[:, :, 1], EPS, None, ALU.add).then_inc(ln_var, 1)
                dve.wait_ge(ln_var, H + 1)
                dve.wait_ge(ln_rs, H + 1)
                link(nc.vector.tensor_tensor(rs_t[:, 0, :], rs_y[:, :], rs_y[:, :], ALU.mult), 3)
                link(nc.vector.tensor_tensor(rs_t[:, 1, :], rs_t[:, 0, :], var4[:, :], ALU.mult), 4)
                link(nc.vector.tensor_scalar(rs_t[:, 0, :], rs_t[:, 1, :], -0.5, 1.5, ALU.mult, ALU.add), 5)
                link(nc.vector.tensor_tensor(rstd[:, :], rs_y[:, :], rs_t[:, 0, :], ALU.mult), 6)
                for i in range(4):
                    last = nc.vector.tensor_scalar(yT[:, half * 4 + i, :], mxp[:, half, i * 128:(i + 1) * 128],
                                                   mv[:, i, 0:1], rstd[:, i:i + 1], ALU.subtract, ALU.mult)
                last.then_inc(ln_y, 1)

            dve.wait_ge(seeded, 1)
            nc.vector.memset(ones[:, :], 1.0)
            for x in (q2, k2):
                nc.vector.memset(x[64:128, :, :, :].bitcast(f32), 1.0)
            nc.vector.memset(qm[64:128, :, :].bitcast(f32), 1.0)
            nc.vector.memset(zeros[:, :], 0.0).then_inc(ready0, 1)
            dve.wait_ge(consts, 80)
            nc.vector.tensor_copy(sel[:, :, :].rearrange("p a n -> p (a n)"), sel_raw)
            dve.wait_ge(ready0, 2)
            nc.vector.tensor_tensor(r_lo[:, :], st_rT, r_hi[:, :].bitcast(f32), ALU.subtract).then_inc(ready0, 1)
            for b in range(BATCH):
                for half in range(2):
                    ln(2 * b + half, half, None)
            dve.wait_ge(ready0, 3)
            dve.wait_ge(lg_done, 1)
            rch = [0]

            def rlink(ins):
                rch[0] += 1
                ins.then_inc(wc_chain, 1)
                dve.wait_ge(wc_chain, rch[0])

            rlink(nc.vector.tensor_copy(lg[:, :, :].rearrange("p t e -> p (t e)"), mxp[:, 0, 0:16 * EXPERTS]))
            l_j = lg[:, :, :].unsqueeze(2).broadcast_to([128, 16, EXPERTS, EXPERTS])
            l_e = lg[:, :, :].unsqueeze(3).broadcast_to([128, 16, EXPERTS, EXPERTS])
            nc.vector.reduce_max(rt3[:, :], lg[:, :, :], AX)
            nc.vector.tensor_tensor(cmp_a, l_j, l_e, ALU.is_equal)
            rlink(nc.vector.tensor_tensor(cmp_b, l_j, l_e, ALU.is_gt))
            rlink(nc.vector.tensor_tensor(cmp_a, cmp_a, tie[:, :, :].unsqueeze(1).broadcast_to([128, 16, EXPERTS, EXPERTS]), ALU.mult))
            rlink(nc.vector.tensor_tensor(cmp_a, cmp_a, cmp_b, ALU.add))
            rlink(nc.vector.tensor_reduce(rt2[:, :, :], cmp_a, AX, ALU.add))
            rlink(nc.vector.tensor_scalar(rt2[:, :, :], rt2[:, :, :], 2.0, None, ALU.is_lt))
            nc.vector.tensor_tensor(rt1[:, :, :], lg[:, :, :], rt3[:, :].unsqueeze(2).broadcast_to([128, 16, EXPERTS]),
                                    ALU.subtract).then_inc(route_ln, 1)
            dve.wait_ge(route_ex, 1)
            rlink(nc.vector.tensor_tensor(rt2[:, :, :], rt2[:, :, :], rt1[:, :, :], ALU.mult))
            rlink(nc.vector.reduce_sum(rt3[:, :], rt2[:, :, :], AX))
            rlink(nc.vector.reciprocal(rt3[:, :], rt3[:, :]))
            nc.vector.tensor_tensor(lg[:, :, :], rt2[:, :, :], rt3[:, :].unsqueeze(2).broadcast_to([128, 16, EXPERTS]),
                                    ALU.mult).then_inc(route_g, 1)
            rlink(nc.vector.memset(gacc, 0.0))
            RC = rch[0]
            with dve.Fori(0, EXPERTS // 2) as ep:
                for s in range(2):
                    e = ep * 2 + s
                    dve.wait_ge(e_in[s], ep * 64 + 64)
                    for tc in range(4):
                        ts = slice(tc * HALF, (tc + 1) * HALF)
                        dve.wait_ge(down_done, e * 4 + tc + 3)
                        dve.wait_ge(mo_acc, e * 4 + tc + 8)
                        nc.vector.scalar_tensor_tensor(e_tmp, acc_bank[tc % 2][:, :], bias_e[:, s, 4:5], gate_b[s][:, ts],
                                                       op0=ALU.add, op1=ALU.mult).then_inc(wc_chain, 1)
                        dve.wait_ge(wc_chain, e * 4 + tc + RC + 1)
                        nc.vector.tensor_tensor(gacc[:, ts], gacc[:, ts], e_tmp, ALU.add).then_inc(mo_acc, 1)
            dve.wait_ge(sig, 1)
            nc.vector.tensor_tensor(gacc, gacc, gate_b[0], ALU.mult).then_inc(gfin, 1)
            WC0 = RC + 4 * EXPERTS

            def lo_half(m, i):
                kq, c = i // 2, i % 2
                cs = slice(c * HALF, (c + 1) * HALF)
                dve.wait_ge(hi_done, 4 * m + i + 1)
                nc.vector.tensor_tensor(kq_lo[:, kq, cs], pj[:, :], kq_hi[:, kq, cs].bitcast(f32), ALU.subtract)\
                    .then_inc(lo_done, 1)

            def max_reduce(m, t):
                half, h, j, c = t // 16, t // 8 % 2, t // 2 % 4, t % 2
                dve.wait_ge(mx_mm, 32 * m + t + 2)
                nc.vector.reduce_max(mx[:, half, h, j, c:c + 1], mxp[:, c, :], AX).then_inc(mx_red, 1)
                if t % 16 == 15:
                    dve.wait_ge(mx_red, 32 * m + t + 3)
                    nc.vector.tensor_tensor(mx_all[:, half, :, :], mx[:, half, :, :, 0], mx[:, half, :, :, 1],
                                            ALU.max).then_inc(m_chain, 1)
                    dve.wait_ge(m_chain, 4 * m + 2 * half + 1)
                    dve.wait_ge(m_row[half], 64 * m + 1)
                    nc.vector.tensor_scalar(m_hl[:, half, :, 0, :], mx_all[:, half, :, :], -1.0, None, ALU.mult).then_inc(m_chain, 1)
                    dve.wait_ge(m_chain, 4 * m + 2 * half + 2)
                    nc.vector.scalar_tensor_tensor(m_hl[:, half, :, 1, :], mx_all[:, half, :, :], -1.0,
                                                   m_hl[:, half, :, 0, :].bitcast(f32), op0=ALU.mult,
                                                   op1=ALU.subtract).then_inc(m_split, 1)

            def unit(g, p, proj2=True, nxt=True):
                n = g * PAIRS + p
                t = 0
                for step in range(16):
                    half, kt = step // 8, step % 8
                    tiles = MX_AT[step] if nxt else 0
                    for _ in range(min(tiles, 2)):
                        max_reduce(n + 1, t)
                        t += 1
                    dve.wait_ge(exp_done, EXP0 + 32 * n + 2 * step + 5)
                    pr, ac = probs[:, 2 * step % 4, :], acc[:, half, 0, :]
                    if kt == 0:
                        dve.wait_ge(sum_mm, 2 * n + half + 2)
                        nc.vector.tensor_copy(ac, pr).then_inc(add_done[0], 1)
                    else:
                        dve.wait_ge(add_done[0], 16 * n + step + 2)
                        nc.vector.tensor_tensor(ac, ac, pr, ALU.add).then_inc(add_done[0], 1)
                    if proj2 and step in PROJ_AT:
                        lo_half(n + 2, PROJ_AT[step])
                    if tiles > 2:
                        max_reduce(n + 1, t)
                        t += 1

            with dve.Fori(0, BATCH) as b:
                with dve.Fori(0, LAYERS) as l:
                    g = b * LAYERS + l
                    n0 = g * PAIRS
                    for half in range(2):
                        hs = slice(half * HALF, (half + 1) * HALF)
                        dve.wait_ge(hh_done, 2 * g + half + 1)
                        nc.vector.tensor_tensor(h_lo[:, hs], hT[:, hs], h_hi[:, hs].bitcast(f32), ALU.subtract).then_inc(hl_done, 1)
                    lo_half(n0, 0)
                    dve.wait_ge(cw_in, 64 * g + 64)
                    for i, (w, uv, o) in enumerate(((st_wk, st_u, wku), (st_wr, st_v, wrv))):
                        nc.vector.tensor_tensor(w, w, uv, ALU.mult).then_inc(wc_chain, 1)
                        lo_half(n0, i + 1)
                        dve.wait_ge(wc_chain, WC0 + 2 * g + i + 1)
                        last = nc.vector.tensor_reduce(o[:, :], w.rearrange("p (h d) -> p h d", d=DH), AX, ALU.add)
                    last.then_inc(wc_done, 1)
                    lo_half(n0, 3)
                    for half in range(2):
                        dve.wait_ge(c_hi_done, 2 * g + half + 1)
                        hs = slice(half * HALF, (half + 1) * HALF)
                        nc.vector.tensor_tensor(c_hl[:, 1, hs], bank[half][0:HEADS, :], c_hl[:, 0, hs].bitcast(f32), ALU.subtract)\
                            .then_inc(c_lo_done, 1)
                    for t in range(18):
                        max_reduce(n0, t)
                    for i in range(4):
                        lo_half(n0 + 1, i)
                        max_reduce(n0, 18 + i)
                    for t in range(22, MX_TILES):
                        max_reduce(n0, t)
                    with dve.Fori(0, 3) as j:
                        unit(g, j * 2)
                        unit(g, j * 2 + 1)
                    with dve.Fori(6, 7) as p:
                        unit(g, p, proj2=False)
                    with dve.Fori(7, 8) as p:
                        unit(g, p, proj2=False, nxt=False)
                    dve.wait_ge(rc_in, 16 * g + 16)
                    nc.vector.reciprocal(rc[:, :], rc[:, :]).then_inc(rc_chain, 1)
                    dve.wait_ge(rc_chain, 2 * g + 1)
                    nc.vector.tensor_copy(rc_hi[:, :], rc[:, :]).then_inc(rc_chain, 1)
                    dve.wait_ge(rc_chain, 2 * g + 2)
                    nc.vector.tensor_tensor(rc_lo[:, :], rc[:, :], rc_hi[:, :].bitcast(f32), ALU.subtract).then_inc(rc_done, 1)
                    dve.wait_ge(pv_ev, 2 * (n0 + PAIRS) + 1)
                    for i in range(2 * PAIRS):
                        v = vecT[:, i // 2, (i % 2) * HALF:(i % 2 + 1) * HALF]
                        dve.wait_ge(bc_mm, 2 * PAIRS * g + i + 1)
                        nc.vector.tensor_tensor(v, bank[i % 4][:, :], v, ALU.mult).then_inc(vec_norm, 1)
                    for half in range(2):
                        hs = slice(half * HALF, (half + 1) * HALF)
                        dve.wait_ge(op_done, 2 * g + half + 2)
                        nc.vector.tensor_tensor(xT[:, hs], acc_bank[half][:, :], hT[:, hs], ALU.add).then_inc(x1_done, 1)
                    for k in range(2):
                        for half in range(2):
                            ln(4 * g + 4 + 2 * k + half, half, None)
                dve.wait_ge(ln_out, 4 * b * LAYERS + 4 * LAYERS + 4)
                dve.wait_ge(fin_in, b * 32 + 32)
                nc.vector.tensor_tensor(st_t0, hT[:, :], st_wk, ALU.mult).then_inc(fin_done, 1)
                dve.wait_ge(fin_done, 2 * b + 3)
                nc.vector.tensor_tensor(st_t0, st_t0, st_wv, ALU.add).then_inc(fin_done, 1)

        @block.gpsimd
        def _(pool):
            pool.wait_ge(seeded, 1)
            pool.wait_ge(ready0, 3)

            def split_w(m):
                pool.wait_ge(wraw_in, 32 * m + 32)
                pool.wait_ge(proj, 4 * m + 1)
                nc.gpsimd.tensor_tensor(w_hi[:, :, :], w_raw[:, :, :], zeros[:, 0:384].rearrange("p (a n) -> p a n", a=3),
                                        ALU.add).then_inc(split_chain, 1)
                pool.wait_ge(split_chain, m + 1)
                nc.gpsimd.tensor_tensor(w_lo[:, :, :], w_raw[:, :, :], w_hi[:, :, :].bitcast(f32), ALU.subtract)\
                    .then_inc(w_split, 1)

            def unit(g, p, split2):
                n = g * PAIRS + p
                for step in range(16):
                    half, kt = step // 8, step % 8
                    pool.wait_ge(exp_done, EXP0 + 32 * n + 2 * step + 6)
                    pr, ac = probs[:, (2 * step + 1) % 4, :], acc[:, half, 1, :]
                    if kt == 0:
                        pool.wait_ge(sum_mm, 2 * n + half + 2)
                        nc.gpsimd.tensor_tensor(ac, pr, zeros[:, :], ALU.add).then_inc(add_done[1], 1)
                    else:
                        pool.wait_ge(add_done[1], 16 * n + step + 2)
                        nc.gpsimd.tensor_tensor(ac, ac, pr, ALU.add).then_inc(add_done[1], 1)
                    if split2 and step == SPLIT_AT:
                        split_w(n + 2)

            with pool.Fori(0, BATCH) as b:
                with pool.Fori(0, LAYERS) as l:
                    g = b * LAYERS + l
                    split_w(g * PAIRS)
                    split_w(g * PAIRS + 1)
                    with pool.Fori(0, 3) as j:
                        unit(g, j * 2, True)
                        unit(g, j * 2 + 1, True)
                    with pool.Fori(6, 7) as p:
                        unit(g, p, False)
                    with pool.Fori(7, 8) as p:
                        unit(g, p, False)


def position_encoding(np):
    pos = np.arange(SEQ - 1, -1, -1, dtype=np.float32)
    freq = np.float32(1.0) / np.power(np.float32(10000.0), np.arange(0, D, 2, dtype=np.float32) / np.float32(D))
    ang = pos[:, None] * freq[None, :].astype(np.float32)
    return np.ascontiguousarray(np.concatenate([np.sin(ang), np.cos(ang)], axis=-1).T.astype(np.float32))


def kernel(**inputs):
    import numpy as np
    import concourse.bacc as bacc
    from concourse import mybir as _mybir
    from concourse.bass_utils import run_bass_kernel_spmd as run

    x = {k.replace("L0_attn_", "").replace("L0_", ""): np.asarray(v) for k, v in inputs.items()}
    c = np.ascontiguousarray
    sel = np.zeros((2 * HEADS, PAIRS, 128), np.float32)
    for r in range(2 * HEADS):
        h = r % HEADS
        sel[r, h // 2, 64 * (h % 2):64 * (h % 2) + 64] = 1.0
    tie = np.zeros((128, EXPERTS, EXPERTS), np.float32)
    for e in range(EXPERTS):
        tie[:, e, :e] = 1.0
    chunks = lambda b, n: b.reshape(b.shape[0], n, 128).transpose(0, 2, 1)
    par = [x[k].reshape(LAYERS, D, 1) for k in ("ln1_g", "ln1_b", "ln2_g", "ln2_b", "b_ff2")]
    arrays = {
        "xT": c(x["x"].reshape(TOK, D).T),
        "ident": np.eye(128, dtype=np.float32),
        "rT": position_encoding(np),
        "sel": sel.reshape(2 * HEADS, PAIRS * 128),
        "tie": tie,
        "W_qkv": c(x["W_qkv"]), "W_r": c(x["W_r"]), "W_o": c(x["W_o"]),
        "W_ff1": c(x["W_ff1"]), "W_ff2": c(x["W_ff2"]),
        "u": c(x["u"].reshape(1, HEADS * DH)), "v": c(x["v"].reshape(1, HEADS * DH)),
        "par": c(np.concatenate(par + [chunks(x["b_ff1"], 4)], axis=2)),
        "w_routerT": c(x["ffn_w_router"].T),
        "w_upT": c(x["ffn_w_up"].transpose(0, 2, 1)),
        "w_downT": c(x["ffn_w_down"].transpose(0, 2, 1)),
        "bias_e": c(np.concatenate([chunks(x["ffn_b_up"], 4), x["ffn_b_down"].reshape(EXPERTS, D, 1)], axis=2)),
    }
    nc = bacc.Bacc("TRN2", target_bir_lowering=False, num_devices=1)
    args = {k: nc.dram_tensor("in_" + k, v.shape, _mybir.dt.from_np(v.dtype), kind="ExternalInput").ap()
            for k, v in arrays.items()}
    out = nc.dram_tensor("out_T", (D, TOK), _mybir.dt.float32, kind="ExternalOutput").ap()
    build(nc, args, out)
    r = run(nc, [{"in_" + k: v for k, v in arrays.items()}], core_ids=[0])
    return c(r.results[0]["out_T"].T).reshape(BATCH, SEQ, D)
```

```python
from contextlib import ExitStack

import concourse.bass as bass
from concourse import mybir

LAYERS, BATCH, SEQ, D, HEADS, DH, FF = 4, 2, 1024, 128, 16, 64, 512
EXPERTS = 8
PAIRS = HEADS // 2
KT = SEQ // 128
HALF = 512
TOK = BATCH * SEQ
MX_TILES = 32
PROJ = [("k", 0), ("k", 1), ("q", 0), ("q", 1)]
PROJ_AT = {6: 0, 8: 1, 11: 2, 13: 3}
MX_AT = ["", "", "", "bc", "abc", "abc", "ab", "abc", "ab", "abc", "abc", "ab", "abc", "ab", "abc", "a"]
FIRST_MX_AT = ["abc", "abc", "ab", "", "", "abc", "abc", "abc", "abc", "abc", "abc", "abc", "abc", "abc", "abc", "ab"]
BEFORE = 24
POOL_BOTH = (4, 5, 9, 11, 12, 14)
DONE = 8 * (HEADS - 2)
RC_AT = 7
SPLIT_AT = 4
EXP0 = 64
TAIL_AT = 1
SUM_AT = 9


def build(nc, a, out_t):
    f32 = mybir.dt.float32
    f32r = mybir.dt.float32r
    ALU = mybir.AluOpType
    ACT = mybir.ActivationFunctionType
    AX = mybir.AxisListType.X
    SCALE = DH ** -0.5
    EPS = 1e-5

    ctx = ExitStack()
    with ctx:
        def sb(name, shape, dt=f32):
            return ctx.enter_context(nc.sbuf_tensor(name, shape, dt))

        def sem(name):
            return ctx.enter_context(nc.semaphore(name))

        xn_dram = nc.dram_tensor("xn_scratch", [BATCH + 1, D, SEQ], f32).ap()
        g_dram = nc.dram_tensor("gate_scratch", [BATCH, D, SEQ], f32).ap()
        route_dram = nc.dram_tensor("route_scratch", [EXPERTS, TOK], f32).ap()
        v_dram = nc.dram_tensor("v_scratch", [KT, 128, HEADS * DH], f32).ap()
        c_dram = nc.dram_tensor("c_scratch", [HEADS, 2, SEQ], f32).ap()
        rowsum_dram = nc.dram_tensor("rowsum_scratch", [PAIRS, 2, SEQ], f32).ap()

        ident = sb("ident", [128, 128])
        r_hi = sb("r_hi", [D, SEQ], f32r)
        r_lo = sb("r_lo", [D, SEQ], f32r)
        sel = sb("sel", [2 * HEADS, PAIRS, 128], f32r)
        ones = sb("ones", [128, 64])
        zeros = sb("zeros", [128, HALF])
        hT = sb("hT", [D, SEQ])
        h_hi = sb("h_hi", [D, SEQ], f32r)
        h_lo = sb("h_lo", [D, SEQ], f32r)
        big = sb("big", [128, 8 * SEQ])
        probs = sb("probs", [128, 4, HALF])
        acc = sb("acc", [128, 2, 2, HALF])
        w_o = sb("w_o", [128, PAIRS, D])
        w_f1 = sb("w_f1", [D, FF])
        w_f2 = sb("w_f2", [128, 4, D])
        par = sb("par", [D, 9])
        q1 = sb("q1", [128, 2, 2, SEQ], f32r)
        q2 = sb("q2", [128, 2, 2, SEQ], f32r)
        k1 = sb("k1", [128, 2, 2, SEQ], f32r)
        k2 = sb("k2", [128, 2, 2, SEQ], f32r)
        qm = sb("qm", [128, 2, SEQ], f32r)
        kq_hi = sb("kq_hi", [128, 2, SEQ], f32r)
        kq_lo = sb("kq_lo", [128, 2, SEQ], f32r)
        v_slot = sb("v_slot", [128, 2, KT, 128])
        w_raw = sb("w_raw", [D, 3, 128])
        w_hi = sb("w_hi", [D, 3, 128], f32r)
        w_lo = sb("w_lo", [D, 3, 128], f32r)
        mx = sb("mx", [128, 2, 2, 4, 2])
        mx_all = sb("mx_all", [128, 2, 2, 4])
        m_hl = sb("m_hl", [128, 2, 2, 2, 4], f32r)
        srow = sb("srow", [128, SEQ])
        rc = sb("rc", [128, 128])
        rcp = sb("rcp", [128, 128])
        rc_hi = sb("rc_hi", [128, 128], f32r)
        rc_lo = sb("rc_lo", [128, 128], f32r)
        rrow = sb("rrow", [2 * HEADS, SEQ], f32r)
        rrow_last = sb("rrow_last", [4, SEQ], f32r)
        sel_last = sb("sel_last", [4, 128], f32r)
        bst = sb("bst", [128, 4, 6])
        mv = sb("mv", [128, 4, 2])
        var4 = sb("var4", [128, 4])
        rs_l = sb("rs_l", [128, 4])
        rs_y = sb("rs_y", [128, 4])
        rs_t = sb("rs_t", [128, 3, 4])
        rstd = sb("rstd", [128, 4])
        c_hl = sb("c_hl", [HEADS, 2, SEQ], f32r)
        wku = sb("wku", [D, HEADS])
        wrv = sb("wrv", [D, HEADS])
        bias_e = sb("bias_e", [128, 2, 5])
        lg = sb("lg", [128, 16, EXPERTS])
        w_rt = sb("w_rt", [D, EXPERTS])
        rt3 = sb("rt3", [128, 16])

        vecT = big[:, :].rearrange("p (a n) -> p a n", a=PAIRS)
        st_wv, st_rT, st_out, st_x, st_wk, st_wr, st_u, st_v = (big[:, SEQ * i:SEQ * (i + 1)] for i in range(8))
        wv_hi, wv_lo = k1[:, 1, 0, :], k1[:, 1, 1, :]
        c_first = [t[:, i, :].bitcast(f32) for t in (kq_hi, kq_lo) for i in range(2)]
        st_val = (st_wk, st_wr, st_u, st_v)
        hid = big[:, 0:4 * SEQ].rearrange("p (f n) -> p f n", f=4)
        flat_acc = acc[:, :, :, :].rearrange("p a b n -> p (a b n)")
        flat_probs = probs[:, :, :].rearrange("p a n -> p (a n)")
        xT = flat_acc[:, 0:SEQ]
        yT = flat_probs[:, 0:SEQ].rearrange("p (t n) -> p t n", n=128)
        xn = big[:, 0:TOK]
        gacc = big[:, TOK:2 * TOK]
        gate_b = [big[:, TOK * (2 + i):TOK * (3 + i)] for i in range(2)]
        e_up = [w_f1[:, :], w_f2[:, :, :].rearrange("p a n -> p (a n)")]
        e_dn = [w_o[:, 0:4, :], w_o[:, 4:8, :]]
        e_h = [probs, acc[:, :, :, :].rearrange("p a b n -> p (a b) n")]
        flat = lambda x: x[:, :, :, :].rearrange("p a b n -> p (a b n)")
        xn_hi, xn_lo = flat(k2)[:, 0:TOK], flat(k2)[:, TOK:2 * TOK]
        e_w = [[flat(q2)[:, (2 * i + j) * SEQ:(2 * i + j + 1) * SEQ] for j in range(2)] for i in range(2)]
        e_hid = [[flat(x)[:, i * TOK:(i + 1) * TOK].rearrange("p (f n) -> p f n", f=4) for x in (q1, k1)] for i in range(2)]
        e_tmp = v_slot[:, 0, 0:4, :].rearrange("p a n -> p (a n)")
        rt1, rt2 = (srow[:, 128 * i:128 * (i + 1)].rearrange("p (t e) -> p t e", t=16) for i in range(2))
        tie = srow[:, 256:256 + EXPERTS * EXPERTS].rearrange("p (e j) -> p e j", e=EXPERTS)
        route_t = v_slot[0:EXPERTS, :, :, :].rearrange("p a b n -> p (a b n)")
        cmp_a = gate_b[0][:, 0:1024].rearrange("p (t e j) -> p t e j", t=16, e=EXPERTS)
        cmp_b = gate_b[0][:, 1024:2048].rearrange("p (t e j) -> p t e j", t=16, e=EXPERTS)
        sel_last_raw = gate_b[1][0:4, 1024:1152]
        sel_raw = gate_b[1][0:2 * HEADS, 0:1024]

        bank = [ctx.enter_context(nc.psum_tensor(f"bank{i}", [128, HALF], f32)) for i in range(4)]
        mxp = ctx.enter_context(nc.psum_tensor("mxp", [128, 2, HALF], f32))
        pv = ctx.enter_context(nc.psum_tensor("pv", [128, HALF], f32))
        pj = ctx.enter_context(nc.psum_tensor("pj", [128, HALF], f32))
        acc_bank = [pv, pj]
        first_bank = [pj, pv, bank[2], bank[3]]

        consts = sem("consts_loaded")
        ready0 = sem("constants_ready")
        seeded = sem("semaphores_seeded")
        x_in = sem("x_loaded")
        ln_t, ln_var, ln_rs, ln_y, ln_b, ln_out = (sem(s) for s in (
            "ln_transposed", "ln_variance", "ln_rstd", "ln_normalised", "ln_back", "ln_out"))
        dve_chain, act_chain = sem("dve_chain"), sem("act_chain")
        xn_out = sem("xn_stored")
        lg_done, route_ln, route_ex, route_g, route_tr, route_cp, route_out = (sem(s) for s in (
            "logits", "route_sub", "route_exp", "route_gates", "route_transposed", "route_copied", "route_stored"))
        e_in = [sem("expert_weights0"), sem("expert_weights1")]
        gate_in = [sem("expert_gate0"), sem("expert_gate1")]
        wv_chain, wv_split = sem("wv_hi_done"), sem("wv_split")
        ones_in = sem("ones_rows_loaded")
        xn_chain, xn_split = sem("xn_hi_done"), sem("xn_split")
        ew_chain, ew_split = sem("expert_hi_done"), sem("expert_split")
        ghi_done, glo_done = sem("gelu_hi_done"), sem("gelu_lo_done")
        up_done, gelu_done, down_done, mo_acc = (sem(s) for s in ("up_done", "gelu_done", "down_done", "expert_added"))
        sig, gfin, g_out = sem("sigmoid_done"), sem("gate_final"), sem("gate_stored")
        h_in = sem("h_loaded")
        cw_in, layer_in, weights_in = sem("c_weights_loaded"), sem("stage_a_loaded"), sem("layer_weights_loaded")
        hh_done, hl_done = sem("h_hi_done"), sem("h_lo_done")
        wc_done, wc_chain = sem("c_weights_done"), sem("c_weights_chain")
        c_mm, c_hi_done, c_lo_done, c_out = sem("c_mm"), sem("c_hi_done"), sem("c_lo_done"), sem("c_stored")
        v_mm, v_ev, v_out = sem("v_mm"), sem("v_evacuated"), [sem(f"v_stored{i}") for i in range(4)]
        wraw_in, w_split, proj = sem("w_raw_loaded"), sem("w_split"), sem("projected")
        hi_done, lo_done = sem("proj_hi_done"), sem("proj_lo_done")
        k2_rows, qm_rows, score_tiles = sem("k2_written"), sem("qm_written"), sem("score_tiles_written")
        v_in = [sem("v_slot_loaded0"), sem("v_slot_loaded1")]
        m_chain, split_chain = sem("m_chain"), sem("w_hi_done")
        mx_mm, mx_red, m_split = sem("max_tile"), sem("max_reduced"), sem("max_split")
        m_row = [sem("m_rows0"), sem("m_rows1")]
        st_done, exp_done, pv_done = sem("scores"), sem("exps"), sem("pv_step")
        add_done = [sem("sum_added0"), sem("sum_added1")]
        pv_ev, sum_mm, sum_cp, sum_out = sem("pv_evacuated"), sem("sum_mm"), sem("sum_copied"), sem("sums_stored")
        rc_in, rc_chain, rc_done = sem("sums_loaded"), sem("rc_chain"), sem("rc_done")
        rrow_in, rrow_last_in = sem("rc_rows"), sem("rc_rows_last")
        bc_mm, vec_norm, op_done, x1_done = sem("rc_broadcast"), sem("vec_normalised"), sem("out_projected"), sem("residual_done")
        f1_mm, f1_act, f2_mm, x2_done = sem("ff1_mm"), sem("ff1_act"), sem("ff2_mm"), sem("ff2_out")
        fin_in, fin_mul, fin_done, res_out = sem("final_loaded"), sem("final_mul"), sem("final_done"), sem("result_stored")
        SEEDS = [(exp_done, EXP0 + 4), (pv_done, 2), (add_done[0], 2), (add_done[1], 2), (sum_cp, 1), (pv_ev, 1),
                 (sum_mm, 3), (sum_out, 1), (k2_rows, 1), (qm_rows, 1), (score_tiles, 1), (mx_mm, 1), (mx_red, 2),
                 (st_done, 1), (op_done, 1), (f2_mm, 1),
                 (proj, 1), (w_split, 1), (m_row[0], 1), (m_row[1], 1),
                 (mo_acc, 8), (gelu_done, 4), (down_done, 2), (fin_done, 2), (res_out, 16)]

        block = ctx.enter_context(nc.Block())

        @block.sync
        def _(sp):
            for s, k in SEEDS:
                sp.sem_inc(s, k)
            sp.sem_inc(seeded, 1)
            sp.dma_start(xT, a["xT"][:, 0:SEQ]).then_inc(x_in, 16)
            sp.dma_start(ident[:, :], a["ident"]).then_inc(consts, 16)
            sp.dma_start(w_rt[:, :], a["w_routerT"]).then_inc(consts, 16)
            sp.dma_start(tie[:, :, :], a["tie"]).then_inc(consts, 16)
            sp.dma_start(st_rT, a["rT"]).then_inc(consts, 16)
            sp.dma_start(sel_raw, a["sel"]).then_inc(consts, 16)
            sp.dma_start(sel_last_raw, a["sel_last"]).then_inc(consts, 16)
            sp.wait_ge(ln_t, 2)
            sp.dma_start(xT, a["xT"][:, SEQ:TOK]).then_inc(x_in, 16)
            for b in range(BATCH):
                sp.wait_ge(ln_out, 2 * (b + 1))
                sp.dma_start(xn_dram[b], xn[:, b * SEQ:(b + 1) * SEQ]).then_inc(xn_out, 16)
            def expert_weights(s, e):
                sp.dma_start(e_up[s], a["w_upT"][e]).then_inc(e_in[s], 16)
                sp.dma_start(e_dn[s], a["w_downT"][e].rearrange("(c p) d -> p c d", p=128)).then_inc(e_in[s], 16)
                sp.dma_start(bias_e[:, s, :], a["bias_e"][e]).then_inc(e_in[s], 16)

            def load_c_weights(l, wk, u, wr, v):
                sp.dma_start(wk, a["W_k"][l]).then_inc(cw_in, 16)
                sp.dma_start(u, a["u"].broadcast_to([128, SEQ])).then_inc(cw_in, 16)
                sp.dma_start(wr, a["W_r_next"][l]).then_inc(cw_in, 16)
                sp.dma_start(v, a["v"].broadcast_to([128, SEQ])).then_inc(cw_in, 16)

            sp.dma_start(xn_dram[BATCH], xn[:, 0:SEQ]).then_inc(xn_out, 16)
            for e in range(2):
                expert_weights(e, e)
            load_c_weights(0, *c_first)
            sp.wait_ge(route_cp, 4)
            sp.dma_start(route_dram, route_t).then_inc(route_out, 16)
            sp.wait_ge(route_out, 16)
            sp.wait_ge(ready0, 3)
            for e in range(2):
                sp.dma_start(gate_b[e], route_dram[e:e + 1, :].broadcast_to([128, TOK])).then_inc(gate_in[e], 16)
            with sp.Fori(1, EXPERTS // 2) as ep:
                for s in range(2):
                    e = ep * 2 + s
                    sp.wait_ge(mo_acc, e * 4 + 4)
                    expert_weights(s, e)
                    sp.dma_start(gate_b[s], route_dram[bass.ds(e, 1), :].broadcast_to([128, TOK])).then_inc(gate_in[s], 16)
            sp.wait_ge(xn_out, 16 * BATCH + 16)
            sp.wait_ge(xn_split, 1)
            sp.wait_ge(lg_done, 1)
            sp.dma_start(hT[:, :], xn_dram[0]).then_inc(h_in, 16)

            def load_w(m, l, p):
                sp.wait_ge(w_split, m + 1)
                sp.wait_ge(seeded, 1)
                sp.dma_start(w_raw[:, 0:2, :], a["W_qkv"][l, :, 0:2 * SEQ].rearrange(
                    "d (t a n) -> d t a n", t=2, n=128)[:, :, p, :]).then_inc(wraw_in, 16)
                sp.dma_start(w_raw[:, 2, :], a["W_r"][l].rearrange("d (a n) -> d a n", n=128)[:, p, :]).then_inc(wraw_in, 16)

            def raw(x):
                return x.bitcast(f32)

            def k2_tile(m, s, c_rows=None):
                sp.wait_ge(lo_done, 4 * m + 2)
                for h in range(2):
                    sp.dma_start(raw(k2[0:64, s, h, :]), raw(kq_hi[64 * h:64 * h + 64, 0, :])).then_inc(k2_rows, 16)
                    if c_rows:
                        c_rows(h)

            def qm_tile(m):
                sp.wait_ge(lo_done, 4 * m + 4)
                sp.wait_ge(mx_mm, 32 * m + 1)
                for h in range(2):
                    sp.dma_start(raw(qm[0:64, h, :]), raw(kq_hi[64 * h:64 * h + 64, 1, :])).then_inc(qm_rows, 16)

            def rest_tiles(s):
                for h in range(2):
                    hs = slice(64 * h, 64 * h + 64)
                    sp.dma_start(raw(k1[0:64, s, h, :]), raw(kq_hi[hs, 0, :])).then_inc(score_tiles, 16)
                    sp.dma_start(raw(k1[64:128, s, h, :]), raw(kq_lo[hs, 0, :])).then_inc(score_tiles, 16)
                    sp.dma_start(raw(q1[0:64, s, h, :]), raw(kq_hi[hs, 1, :])).then_inc(score_tiles, 16)
                    sp.dma_start(raw(q1[64:128, s, h, :]), raw(kq_hi[hs, 1, :])).then_inc(score_tiles, 16)
                    sp.dma_start(raw(q2[0:64, s, h, :]), raw(kq_lo[hs, 1, :])).then_inc(score_tiles, 16)

            def load_v(g, m, p, s):
                sp.dma_start(v_slot[:, s, :, :], v_dram.rearrange(
                    "t k (a n) -> k t a n", n=128)[:, :, p, :]).then_inc(v_in[s], 16)

            def m_rows(m, s, half):
                sp.wait_ge(m_split, 2 * m + half + 1)
                for h in range(2):
                    for i in range(2):
                        sp.dma_start(raw(q2[66 + i:67 + i, s, h, half * HALF:(half + 1) * HALF]),
                                     raw(m_hl[:, half, h, i, :])).then_inc(m_row[half], 16)

            def store_sums(n, p):
                sp.wait_ge(sum_cp, 2 * n + 3)
                sp.wait_ge(seeded, 1)
                for h in range(2):
                    sp.dma_start(rowsum_dram.rearrange("a h n -> h a n")[h, p, :], srow[64 * h:64 * h + 1, :]).then_inc(sum_out, 16)

            def unit(g, l, p, s, prev=True, proj2=True, nxt=True):
                n = g * PAIRS + p
                if nxt:
                    qm_tile(n + 1)
                if not prev:
                    m_rows(n, s, 1)
                if proj2 and prev:
                    load_w(n + 2, l, p + 2)
                if nxt and prev:
                    sp.wait_ge(pv_done, 16 * n + 2)
                    rest_tiles(1 - s)
                if nxt:
                    load_v(g, n + 1, p + 1, 1 - s)
                if prev:
                    store_sums(n - 1, p - 1)
                if nxt:
                    m_rows(n + 1, 1 - s, 0)
                if proj2:
                    sp.wait_ge(st_done, 32 * n + 33)
                    k2_tile(n + 2, s, c_from_dram(p + 2, s))
                if nxt:
                    m_rows(n + 1, 1 - s, 1)

            def c_from_dram(p, s):
                return lambda h: sp.dma_start(raw(k2[64:66, s, h, :]), c_dram[2 * p + h]).then_inc(k2_rows, 16)

            sp.wait_ge(down_done, 4 * EXPERTS + 2)
            for i in range(2):
                sp.dma_start(raw(k2[66:68, i, :, :]), raw(qm[64:66, :, :])).then_inc(ones_in, 16)
                sp.dma_start(raw(q2[64:66, i, :, :]), raw(qm[64:66, :, :])).then_inc(ones_in, 16)
            with sp.Fori(0, BATCH) as b:
                with sp.Fori(0, LAYERS) as l:
                    g = b * LAYERS + l
                    load_w(g * PAIRS, l, 0)
                    sp.wait_ge(f2_mm, 2 * g + 1)
                    sp.wait_ge(seeded, 1)
                    sp.dma_start(st_rT, a["rT"]).then_inc(layer_in, 16)
                    load_w(g * PAIRS + 1, l, 1)
                    sp.dma_start(st_wv, a["W_qkv"][l, :, 2 * SEQ:3 * SEQ]).then_inc(layer_in, 16)
                    sp.wait_ge(gfin, 1)
                    sp.wait_ge(seeded, 1)
                    sp.dma_start(w_o[:, :, :], a["W_o"][l].rearrange("(a p) d -> p a d", p=128)).then_inc(weights_in, 16)
                    sp.dma_start(w_f1[:, :], a["W_ff1"][l]).then_inc(weights_in, 16)
                    sp.dma_start(w_f2[:, :, :], a["W_ff2"][l].rearrange("(c p) d -> p c d", p=128)).then_inc(weights_in, 16)
                    sp.wait_ge(ln_out, 4 * g + 4)
                    sp.wait_ge(seeded, 1)
                    sp.dma_start(par[:, :], a["par"][l]).then_inc(weights_in, 16)

                    sp.wait_ge(ones_in, 64)
                    k2_tile(g * PAIRS, 0)
                    qm_tile(g * PAIRS)
                    sp.wait_ge(c_lo_done, 2 * g + 2)
                    sp.wait_ge(c_hi_done, 2 * g + 2)
                    for h in range(2):
                        sp.dma_start(raw(k2[64:66, 0, h, :]), raw(c_hl[h:h + 1, :, :])).then_inc(k2_rows, 16)
                    rest_tiles(0)
                    sp.dma_start(c_dram[:, 0, :], raw(c_hl[:, 0, :])).then_inc(c_out, 16)
                    sp.dma_start(c_dram[:, 1, :], raw(c_hl[:, 1, :])).then_inc(c_out, 16)
                    sp.wait_ge(c_out, 32 * g + 32)
                    sp.wait_ge(g_out, 16 * BATCH)
                    sp.wait_ge(res_out, 16 * b + 16)
                    m_rows(g * PAIRS, 0, 0)
                    for i in range(4):
                        sp.wait_ge(v_out[i], 32 * g + 32)
                    load_v(g, g * PAIRS, 0, 0)
                    k2_tile(g * PAIRS + 1, 1, c_from_dram(1, 1))
                    sp.wait_ge(lo_done, 4 * (g * PAIRS + 1) + 4)
                    rest_tiles(1)
                    load_w(g * PAIRS + 2, l, 2)
                    with sp.Fori(0, 1) as p:
                        unit(g, l, p, 0, prev=False)
                    with sp.Fori(0, 2) as j:
                        unit(g, l, j * 2 + 1, 1)
                        unit(g, l, j * 2 + 2, 0)
                    with sp.Fori(5, 6) as p:
                        unit(g, l, p, 1)
                    with sp.Fori(6, 7) as p:
                        unit(g, l, p, 0, proj2=False)
                    with sp.Fori(7, 8) as p:
                        unit(g, l, p, 1, proj2=False, nxt=False)
                    sp.wait_ge(sum_out, 32 * (g * PAIRS + 7) + 1)
                    sp.dma_start(rc[0:DONE, :], rowsum_dram.rearrange("a h (c n) -> (a h c) n", n=128)[0:DONE, :]).then_inc(rc_in, 16)
                    sp.wait_ge(rc_done, 2 * g + 1)
                    sp.dma_start(raw(rrow[0:HEADS - 2, :]), raw(rc_hi[0:DONE, :])).then_inc(rrow_in, 16)
                    sp.dma_start(raw(rrow[HEADS:2 * HEADS - 2, :]), raw(rc_lo[0:DONE, :])).then_inc(rrow_in, 16)
                    store_sums(g * PAIRS + 7, 7)
                    sp.wait_ge(sum_out, 32 * (g * PAIRS + 8) + 1)
                    sp.dma_start(rc[DONE:128, :], rowsum_dram.rearrange("a h (c n) -> (a h c) n", n=128)[DONE:128, :]).then_inc(rc_in, 16)
                    sp.wait_ge(rc_done, 2 * g + 2)
                    sp.dma_start(raw(rrow_last[0:2, :]), raw(rc_hi[DONE:128, :])).then_inc(rrow_last_in, 16)
                    sp.dma_start(raw(rrow_last[2:4, :]), raw(rc_lo[DONE:128, :])).then_inc(rrow_last_in, 16)
                    sp.wait_ge(op_done, 2 * g + 3)
                    sp.wait_ge(seeded, 1)
                    load_c_weights(l + 1, st_wk, st_u, st_wr, st_v)
                sp.wait_ge(f2_mm, 2 * b * LAYERS + 2 * LAYERS + 1)
                sp.wait_ge(seeded, 1)
                sp.dma_start(st_x, a["xT"].rearrange("d (b n) -> d b n", b=BATCH)[:, b, :]).then_inc(fin_in, 16)
                sp.dma_start(st_wv, g_dram[b]).then_inc(fin_in, 16)
                sp.wait_ge(fin_done, 2 * b + 3)
                sp.wait_ge(seeded, 1)
                sp.dma_start(hT[:, :], xn_dram[b + 1]).then_inc(h_in, 16)
                sp.wait_ge(fin_done, 2 * b + 4)
                sp.wait_ge(seeded, 1)
                sp.dma_start(out_t.rearrange("d (b n) -> d b n", b=BATCH)[:, b, :], st_out).then_inc(res_out, 16)
            sp.wait_ge(res_out, BATCH * 16 + 16)
            sp.wait_ge(h_in, BATCH * 16 + 16)

        @block.tensor
        def _(pe):
            def ln(H, half):
                for i in range(4):
                    t = half * 4 + i
                    last = nc.tensor.transpose(mxp[:, half, i * 128:(i + 1) * 128], xT[:, t * 128:(t + 1) * 128], ident[:, :])
                last.then_inc(ln_t, 1)

            def ln_back(H, half):
                pe.wait_ge(ln_y, H + 1)
                for i in range(4):
                    last = nc.tensor.transpose(mxp[:, half, i * 128:(i + 1) * 128], yT[:, half * 4 + i, :], ident[:, :])
                last.then_inc(ln_b, 1)

            pe.wait_ge(seeded, 1)
            pe.wait_ge(consts, 96)
            for b in range(BATCH):
                pe.wait_ge(x_in, 16 * (b + 1))
                for half in range(2):
                    if b:
                        pe.wait_ge(ln_out, half + 1)
                    ln(2 * b + half, half)
                for half in range(2):
                    ln_back(2 * b + half, half)
            pe.wait_ge(ln_out, 4)
            for t in range(16):
                last = nc.tensor.matmul(mxp[:, 0, t * EXPERTS:(t + 1) * EXPERTS], xn[:, t * 128:(t + 1) * 128],
                                        w_rt[:, :], start=True, stop=True)
            last.then_inc(lg_done, 1)
            pe.wait_ge(route_g, 1)
            for t in range(16):
                last = nc.tensor.transpose(bank[t // 4][0:EXPERTS, (t % 4) * 128:(t % 4 + 1) * 128], lg[:, t, :], ident[:, :])
                if t % 4 == 3:
                    last.then_inc(route_tr, 1)
            pe.wait_ge(route_cp, 4)

            pe.wait_ge(xn_split, 1)
            with pe.Fori(0, EXPERTS // 2) as ep:
                def up(u):
                    s, tc = u // 4, u % 4
                    ts = slice(tc * HALF, (tc + 1) * HALF)
                    if tc == 0:
                        pe.wait_ge(ew_split, ep * 4 + s * 2 + 2)
                    for f in range(4):
                        pe.wait_ge(gelu_done, ep * 32 + u * 4 + f + 1)
                        fs = slice(f * 128, (f + 1) * 128)
                        nc.tensor.matmul(bank[f][:, :], e_w[s][0][:, fs], xn_hi[:, ts], start=True, stop=False)
                        nc.tensor.matmul(bank[f][:, :], e_w[s][0][:, fs], xn_lo[:, ts], start=False, stop=False)
                        nc.tensor.matmul(bank[f][:, :], e_w[s][1][:, fs], xn_hi[:, ts], start=False, stop=True)\
                            .then_inc(up_done, 1)

                def down(u):
                    s, tc = u // 4, u % 4
                    pe.wait_ge(mo_acc, ep * 8 + u + 7)
                    pe.wait_ge(glo_done, ep * 32 + u * 4 + 4)
                    hi, lo = e_hid[tc % 2]
                    for f in range(4):
                        fs = slice(HALF + f * 128, HALF + (f + 1) * 128)
                        nc.tensor.matmul(acc_bank[tc % 2][:, :], e_w[s][0][:, fs], hi[:, f, :], start=(f == 0), stop=False)
                        nc.tensor.matmul(acc_bank[tc % 2][:, :], e_w[s][0][:, fs], lo[:, f, :], start=False, stop=False)
                        last = nc.tensor.matmul(acc_bank[tc % 2][:, :], e_w[s][1][:, fs], hi[:, f, :],
                                                start=False, stop=(f == 3))
                    last.then_inc(down_done, 1)

                up(0)
                for u in range(8):
                    if u < 7:
                        up(u + 1)
                    down(u)

            def project(m, i, after=(), dst=pj):
                kind, c = PROJ[i]
                if i in after:
                    pe.wait_ge(lo_done, 4 * m + i)
                cols = slice(c * HALF, (c + 1) * HALF)
                w = 1 if kind == "k" else 0
                ops = [(w_hi, w, h_hi), (w_hi, w, h_lo), (w_lo, w, h_hi)]
                if kind == "k":
                    ops += [(w_hi, 2, r_hi), (w_hi, 2, r_lo), (w_lo, 2, r_hi)]
                for j, (wt, k, x) in enumerate(ops):
                    last = nc.tensor.matmul(dst[:, :], wt[:, k, :], x[:, cols], start=(j == 0), stop=(j == len(ops) - 1))
                last.then_inc(proj, 1)

            def max_tile(m, s, t):
                if t == 0:
                    pe.wait_ge(k2_rows, 64 * m + 65)
                    pe.wait_ge(qm_rows, 32 * m + 33)
                half, h, j, c = t // 16, t // 8 % 2, t // 2 % 4, t % 2
                pe.wait_ge(mx_red, 32 * m + t + 1)
                w = qm[0:66, h, half * HALF:(half + 1) * HALF].rearrange("p (q j) -> p j q", j=4)[:, j, :]
                nc.tensor.matmul(mxp[:, c, :], w, k2[0:66, s, h, c * HALF:(c + 1) * HALF],
                                 start=True, stop=True).then_inc(mx_mm, 1)

            def scores(n, s, i):
                half, kt, h = i // 16, i // 2 % 8, i % 2
                if i % 16 == 0:
                    pe.wait_ge(m_row[half], 64 * n + 65)
                    pe.wait_ge(score_tiles, 160 * n + 161)
                pe.wait_ge(exp_done, EXP0 + 32 * n + i + 1)
                ks, qs = slice(kt * 128, (kt + 1) * 128), slice(half * HALF, (half + 1) * HALF)
                nc.tensor.matmul(bank[i % 4][:, :], k1[:, s, h, ks], q1[:, s, h, qs], start=True, stop=False)
                nc.tensor.matmul(bank[i % 4][:, :], k2[0:68, s, h, ks], q2[0:68, s, h, qs],
                                 start=False, stop=True).then_inc(st_done, 1)

            def sums(n, half):
                for h in range(2):
                    pe.wait_ge(add_done[h], 16 * n + 8 * half + 10)
                    last = nc.tensor.matmul(pj[64 * h:64 * h + 64, :], ones[:, :], acc[:, half, h, :], start=True, stop=True)
                last.then_inc(sum_mm, 1)

            def unit(g, p, s, prev=True, proj2=True, nxt=True):
                n = g * PAIRS + p
                queue = iter([(n + 1, 1 - s, t) for t in range(MX_TILES)] if prev else
                             [(n, s, t) for t in range(BEFORE, MX_TILES)] + [(n + 1, 1 - s, t) for t in range(MX_TILES)])
                for step in range(16):
                    half, kt = step // 8, step % 8
                    tiles = (MX_AT[step] if prev else FIRST_MX_AT[step]) if nxt else ""
                    if proj2 and step in PROJ_AT:
                        i = PROJ_AT[step]
                        if i == 0:
                            pe.wait_ge(w_split, n + 4)
                            pe.wait_ge(sum_cp, 2 * n + 1)
                        if i == 2:
                            pe.wait_ge(sum_cp, 2 * n + 2)
                        project(n + 2, i, after=(1, 3))
                    if "a" in tiles:
                        max_tile(*next(queue))
                    if step < 15:
                        scores(n, s, 2 * step + 2)
                        scores(n, s, 2 * step + 3)
                    elif nxt:
                        scores(n + 1, 1 - s, 0)
                        scores(n + 1, 1 - s, 1)
                    if "b" in tiles:
                        max_tile(*next(queue))
                    if kt == 0:
                        pe.wait_ge(pv_ev, 2 * n + half + 1)
                    if step == 0:
                        pe.wait_ge(v_in[s], 8 * n - 8 * s + 16)
                    for h in range(2):
                        i = 2 * step + h
                        pe.wait_ge(exp_done, EXP0 + 32 * n + i + 5)
                        last = nc.tensor.matmul(pv[64 * h:64 * h + 64, :], v_slot[:, s, kt, 64 * h:64 * h + 64],
                                                probs[:, i % 4, :], start=(kt == 0), stop=(kt == 7))
                    last.then_inc(pv_done, 1)
                    for _ in range(tiles.count("c")):
                        max_tile(*next(queue))
                    if prev and step == TAIL_AT:
                        if nxt:
                            pe.wait_ge(lo_done, 4 * n + 8)
                        pe.wait_ge(sum_cp, 2 * n)
                        sums(n - 1, 1)
                    if step == SUM_AT:
                        if proj2:
                            pe.wait_ge(lo_done, 4 * n + 10)
                        pe.wait_ge(sum_cp, 2 * n + 1)
                        sums(n, 0)

            with pe.Fori(0, BATCH) as b:
                with pe.Fori(0, LAYERS) as l:
                    g = b * LAYERS + l
                    n0 = g * PAIRS
                    pe.wait_ge(ln_out, 4 * g + 4)
                    pe.wait_ge(w_split, n0 + 2)
                    for i in range(4):
                        if i < 2:
                            pe.wait_ge(hh_done, 2 * g + i + 1)
                            pe.wait_ge(hl_done, 2 * g + i + 1)
                        project(n0, i, dst=first_bank[i])
                    pe.wait_ge(layer_in, 32 * g + 32)
                    pe.wait_ge(wc_done, g + 1)
                    for half in range(2):
                        hs = slice(half * HALF, (half + 1) * HALF)
                        nc.tensor.matmul(bank[half][0:HEADS, :], wku[:, :], hT[:, hs], start=True, stop=False)
                        nc.tensor.matmul(bank[half][0:HEADS, :], wrv[:, :], st_rT[:, hs], start=False, stop=True)\
                            .then_inc(c_mm, 1)
                    pe.wait_ge(wv_split, g + 1)
                    t = 0
                    for i in range(16):
                        if i >= 4:
                            pe.wait_ge(v_ev, 16 * g + i - 3)
                        b_i = (i + 2) % 4
                        if i in (2, 3):
                            pe.wait_ge(c_lo_done, 2 * g + i - 1)
                        if i in (0, 1):
                            pe.wait_ge(lo_done, 4 * n0 + i + 3)
                        ks, cs = slice((i // 2) * 128, (i // 2 + 1) * 128), slice((i % 2) * HALF, (i % 2 + 1) * HALF)
                        nc.tensor.matmul(bank[b_i][:, :], h_hi[:, ks], wv_hi[:, cs], start=True, stop=False)
                        nc.tensor.matmul(bank[b_i][:, :], h_hi[:, ks], wv_lo[:, cs], start=False, stop=False)
                        nc.tensor.matmul(bank[b_i][:, :], h_lo[:, ks], wv_hi[:, cs], start=False, stop=True).then_inc(v_mm, 1)
                        if i >= 8:
                            for _ in range(2):
                                max_tile(n0, 0, t)
                                t += 1
                    pe.wait_ge(w_split, n0 + 3)
                    for i in range(4):
                        pe.wait_ge(lo_done, 4 * (n0 + 1) + max(i - 1, 0))
                        project(n0 + 1, i, dst=acc_bank[1 - i % 2])
                        for _ in range(2):
                            max_tile(n0, 0, t)
                            t += 1
                    pe.wait_ge(v_ev, 16 * g + 16)
                    pe.wait_ge(lo_done, 4 * (n0 + 1) + 4)
                    scores(n0, 0, 0)
                    scores(n0, 0, 1)
                    with pe.Fori(0, 1) as p:
                        unit(g, p, 0, prev=False)
                    with pe.Fori(0, 2) as j:
                        unit(g, j * 2 + 1, 1)
                        unit(g, j * 2 + 2, 0)
                    with pe.Fori(5, 6) as p:
                        unit(g, p, 1)
                    with pe.Fori(6, 7) as p:
                        unit(g, p, 0, proj2=False)
                    with pe.Fori(7, 8) as p:
                        unit(g, p, 1, proj2=False, nxt=False)
                    pe.wait_ge(sum_cp, 2 * (n0 + 7) + 2)
                    sums(n0 + 7, 1)
                    pe.wait_ge(rrow_in, 32 * g + 32)
                    pe.wait_ge(exp_done, EXP0 + 32 * (n0 + PAIRS) + 4)
                    for i in range(2 * PAIRS + 3):
                        if i < 2 * PAIRS:
                            if i >= 4:
                                pe.wait_ge(vec_norm, 2 * PAIRS * g + i - 3)
                            hs = slice((i % 2) * HALF, (i % 2 + 1) * HALF)
                            if i < 2 * PAIRS - 2:
                                nc.tensor.matmul(bank[i % 4][:, :], sel[:, i // 2, :], rrow[:, hs],
                                                 start=True, stop=True).then_inc(bc_mm, 1)
                            else:
                                if i == 2 * PAIRS - 2:
                                    pe.wait_ge(rrow_last_in, 32 * g + 32)
                                nc.tensor.matmul(bank[i % 4][:, :], sel_last[:, :], rrow_last[:, hs],
                                                 start=True, stop=True).then_inc(bc_mm, 1)
                        if i == 3:
                            pe.wait_ge(weights_in, 64 * g + 64)
                            pe.wait_ge(sum_cp, 2 * (n0 + PAIRS) + 1)
                            pe.wait_ge(pv_ev, 2 * (n0 + PAIRS) + 1)
                        if i >= 3:
                            o = i - 3
                            pe.wait_ge(vec_norm, 2 * PAIRS * g + o + 1)
                            last = nc.tensor.matmul(acc_bank[o % 2][:, :], w_o[:, o // 2, :],
                                                    vecT[:, o // 2, (o % 2) * HALF:(o % 2 + 1) * HALF],
                                                    start=(o < 2), stop=(o >= 2 * PAIRS - 2))
                            if o >= 2 * PAIRS - 2:
                                last.then_inc(op_done, 1)
                    H = 4 * g + 4
                    for half in range(2):
                        pe.wait_ge(x1_done, 2 * g + half + 1)
                        ln(H + half, half)

                    def ff1(half):
                        pe.wait_ge(ln_out, H + half + 1)
                        for f in range(4):
                            if half:
                                pe.wait_ge(f1_act, 8 * g + f + 1)
                            nc.tensor.matmul(bank[f][:, :], w_f1[:, f * 128:(f + 1) * 128],
                                             hT[:, half * HALF:(half + 1) * HALF], start=True, stop=True).then_inc(f1_mm, 1)

                    def ff2(half):
                        pe.wait_ge(f1_act, 8 * g + 4 * half + 4)
                        hs = slice(half * HALF, (half + 1) * HALF)
                        for f in range(4):
                            last = nc.tensor.matmul(acc_bank[half][:, :], w_f2[:, f, :], hid[:, f, hs], start=(f == 0), stop=(f == 3))
                        last.then_inc(f2_mm, 1)

                    ln_back(H, 0)
                    ff1(0)
                    ln_back(H + 1, 1)
                    ff2(0)
                    ff1(1)
                    pe.wait_ge(x2_done, 2 * g + 1)
                    ln(H + 2, 0)
                    ff2(1)
                    ln_back(H + 2, 0)
                    pe.wait_ge(x2_done, 2 * g + 2)
                    ln(H + 3, 1)
                    ln_back(H + 3, 1)

        @block.scalar
        def _(act):
            def ln(H):
                act.wait_ge(ln_var, H + 1)
                nc.scalar.activation(rs_l[:, :], var4[:, :], ACT.Ln).then_inc(act_chain, 1)
                act.wait_ge(act_chain, H + 1)
                nc.scalar.activation(rs_y[:, :], rs_l[:, :], ACT.Exp, scale=-0.5).then_inc(ln_rs, 1)

            def ln_finish(H, half, out, scale=1.0, bias=0.0):
                act.wait_ge(ln_b, H + 1)
                nc.scalar.activation(out, mxp[:, half, :], ACT.Identity, scale=scale, bias=bias).then_inc(ln_out, 1)

            act.wait_ge(seeded, 1)
            nc.scalar.preload_act_table_set("natural_log_exp_and_others")
            act.wait_ge(consts, 96)
            nc.scalar.activation(r_hi[:, :], st_rT, ACT.Copy).then_inc(ready0, 1)
            for b in range(BATCH):
                for half in range(2):
                    ln(2 * b + half)
                for half in range(2):
                    ln_finish(2 * b + half, half, xn[:, b * SEQ + half * HALF:b * SEQ + (half + 1) * HALF])
            act.wait_ge(route_ln, 1)
            nc.scalar.activation(rt1[:, :, :], rt1[:, :, :], ACT.Exp).then_inc(route_ex, 1)
            for i in range(4):
                act.wait_ge(route_tr, i + 1)
                nc.scalar.activation(route_t[:, i * HALF:(i + 1) * HALF], bank[i][0:EXPERTS, :], ACT.Copy).then_inc(route_cp, 1)
            with act.Fori(0, EXPERTS // 2) as ep:
                for s in range(2):
                    e = ep * 2 + s
                    act.wait_ge(e_in[s], ep * 48 + 48)
                    for tc in range(4):
                        act.wait_ge(down_done, e * 4 + tc + 1)
                        for f in range(5):
                            if f < 4:
                                act.wait_ge(up_done, (e * 4 + tc) * 4 + f + 1)
                                nc.scalar.activation(e_h[tc % 2][:, f, :], bank[f][:, :], ACT.Gelu,
                                                     bias=bias_e[:, s, f:f + 1]).then_inc(gelu_done, 1)
                            if f > 0:
                                act.wait_ge(gelu_done, (e * 4 + tc) * 4 + f + 4)
                                nc.scalar.activation(e_hid[tc % 2][0][:, f - 1, :], e_h[tc % 2][:, f - 1, :], ACT.Copy)\
                                    .then_inc(ghi_done, 1)
            act.wait_ge(mo_acc, 4 * EXPERTS + 8)
            nc.scalar.activation(gate_b[0], gacc, ACT.Sigmoid).then_inc(sig, 1)

            def hi_half(m, i, src=pj):
                kq, c = i // 2, i % 2
                if i == 0:
                    act.wait_ge(k2_rows, 64 * m + 1)
                    act.wait_ge(qm_rows, 32 * m + 1)
                    act.wait_ge(score_tiles, 160 * m + 1)
                act.wait_ge(proj, 4 * m + i + 2)
                nc.scalar.activation(kq_hi[:, kq, c * HALF:(c + 1) * HALF], src[:, :], ACT.Copy).then_inc(hi_done, 1)

            def unit(g, p, prev=True, proj2=True):
                n = g * PAIRS + p
                for step in range(16):
                    act.wait_ge(pv_done, 16 * n + step + 1)
                    for h in range(2):
                        act.wait_ge(add_done[h], 16 * n + step + 1)
                        i = 2 * step + h
                        act.wait_ge(st_done, 32 * n + i + 2)
                        nc.scalar.activation(probs[:, i % 4, :], bank[i % 4][:, :], ACT.Exp, scale=SCALE).then_inc(exp_done, 1)
                    if prev and step == 0:
                        evacuate(n - 1, p - 1, 1)
                    if step == 8:
                        evacuate(n, p, 0)
                    if proj2 and step in PROJ_AT:
                        hi_half(n + 2, PROJ_AT[step])
                    if prev and step == TAIL_AT + 1:
                        sum_copy(n - 1, 1)
                    if step == SUM_AT + 1:
                        sum_copy(n, 0)

            def evacuate(n, p, half):
                act.wait_ge(pv_done, 16 * n + 8 * half + 10)
                nc.scalar.activation(big[:, bass.ds(p * SEQ + half * HALF, HALF)], pv[:, :], ACT.Copy).then_inc(pv_ev, 1)

            def sum_copy(n, half):
                act.wait_ge(sum_mm, 2 * n + half + 4)
                if half == 0:
                    act.wait_ge(sum_out, 32 * n + 1)
                nc.scalar.activation(srow[:, half * HALF:(half + 1) * HALF], pj[:, :], ACT.Copy).then_inc(sum_cp, 1)

            nc.scalar.preload_act_table_set("natural_log_exp_and_others")
            act.wait_ge(gfin, 1)
            for b in range(BATCH):
                act.dma_start(g_dram[b], gacc[:, b * SEQ:(b + 1) * SEQ]).then_inc(g_out, 16)
            with act.Fori(0, BATCH) as b:
                with act.Fori(0, LAYERS) as l:
                    g = b * LAYERS + l
                    n0 = g * PAIRS
                    act.wait_ge(h_in, b * 16 + 16)
                    act.wait_ge(ln_out, 4 * g + 4)
                    for half in range(2):
                        hs = slice(half * HALF, (half + 1) * HALF)
                        nc.scalar.activation(h_hi[:, hs], hT[:, hs], ACT.Copy).then_inc(hh_done, 1)
                    for i in range(4):
                        hi_half(n0, i, first_bank[i])
                    for half in range(2):
                        act.wait_ge(c_mm, 2 * g + half + 1)
                        nc.scalar.activation(c_hl[:, 0, half * HALF:(half + 1) * HALF], bank[half][0:HEADS, :], ACT.Copy)\
                            .then_inc(c_hi_done, 1)
                    for i in range(16):
                        t, c = i // 2, i % 2
                        act.wait_ge(v_mm, 16 * g + i + 1)
                        if t >= 4 and c == 0:
                            act.wait_ge(v_out[t % 4], 32 * g + 16)
                        nc.scalar.activation(st_val[t % 4][:, c * HALF:(c + 1) * HALF], bank[(i + 2) % 4][:, :],
                                             ACT.Copy).then_inc(v_ev, 1)
                        if c:
                            act.wait_ge(v_ev, 16 * g + i + 1)
                            act.dma_start(v_dram[t], st_val[t % 4]).then_inc(v_out[t % 4], 16)
                    for i in range(4):
                        hi_half(n0 + 1, i, acc_bank[1 - i % 2])
                    with act.Fori(0, 1) as p:
                        unit(g, p, prev=False)
                    with act.Fori(0, 4) as j:
                        unit(g, j + 1)
                    with act.Fori(5, 6) as p:
                        unit(g, p)
                    with act.Fori(6, 7) as p:
                        unit(g, p, proj2=False)
                    with act.Fori(7, 8) as p:
                        unit(g, p, proj2=False)
                    evacuate(n0 + 7, 7, 1)
                    sum_copy(n0 + 7, 1)
                    H = 4 * g + 4
                    act.wait_ge(weights_in, 64 * g + 64)
                    for half in range(2):
                        ln(H + half)

                    def relu(half):
                        hs = slice(half * HALF, (half + 1) * HALF)
                        for f in range(4):
                            act.wait_ge(f1_mm, 8 * g + 4 * half + f + 1)
                            nc.scalar.activation(hid[:, f, hs], bank[f][:, :], ACT.Relu, bias=par[:, 5 + f:6 + f])\
                                .then_inc(f1_act, 1)

                    def ff_out(half):
                        act.wait_ge(f2_mm, 2 * g + half + 2)
                        nc.scalar.activation(xT[:, half * HALF:(half + 1) * HALF], acc_bank[half][:, :], ACT.Identity,
                                             bias=par[:, 4:5]).then_inc(x2_done, 1)

                    ln_finish(H, 0, hT[:, 0:HALF], par[:, 0:1], par[:, 1:2])
                    relu(0)
                    ln_finish(H + 1, 1, hT[:, HALF:SEQ], par[:, 0:1], par[:, 1:2])
                    ff_out(0)
                    relu(1)
                    ln(H + 2)
                    ff_out(1)
                    ln_finish(H + 2, 0, hT[:, 0:HALF], par[:, 2:3], par[:, 3:4])
                    ln(H + 3)
                    ln_finish(H + 3, 1, hT[:, HALF:SEQ], par[:, 2:3], par[:, 3:4])

        @block.vector
        def _(dve):
            def ln(H, half):
                def link(ins, k):
                    ins.then_inc(dve_chain, 1)
                    dve.wait_ge(dve_chain, H * 6 + k)
                dve.wait_ge(ln_t, H + 1)
                for i in range(4):
                    last = nc.vector.bn_stats(bst[:, i, :], mxp[:, half, i * 128:(i + 1) * 128])
                link(last, 1)
                nc.vector.memset(rs_t[:, 2, :], 0.0)
                for i in range(4):
                    last = nc.vector.bn_aggr(mv[:, i, :], bst[:, i, :])
                link(last, 2)
                nc.vector.tensor_scalar(var4[:, :], mv[:, :, 1], EPS, None, ALU.add).then_inc(ln_var, 1)
                dve.wait_ge(ln_var, H + 1)
                dve.wait_ge(ln_rs, H + 1)
                link(nc.vector.tensor_tensor(rs_t[:, 0, :], rs_y[:, :], rs_y[:, :], ALU.mult), 3)
                link(nc.vector.tensor_tensor(rs_t[:, 1, :], rs_t[:, 0, :], var4[:, :], ALU.mult), 4)
                link(nc.vector.tensor_scalar(rs_t[:, 0, :], rs_t[:, 1, :], -0.5, 1.5, ALU.mult, ALU.add), 5)
                link(nc.vector.tensor_tensor(rstd[:, :], rs_y[:, :], rs_t[:, 0, :], ALU.mult), 6)
                for i in range(4):
                    last = nc.vector.tensor_scalar(yT[:, half * 4 + i, :], mxp[:, half, i * 128:(i + 1) * 128],
                                                   mv[:, i, 0:1], rstd[:, i:i + 1], ALU.subtract, ALU.mult)
                last.then_inc(ln_y, 1)

            dve.wait_ge(seeded, 1)
            nc.vector.memset(ones[:, :], 1.0)
            nc.vector.memset(rrow[:, :].bitcast(f32), 0.0)
            nc.vector.memset(qm[64:128, :, :].bitcast(f32), 1.0)
            nc.vector.memset(zeros[:, :], 0.0).then_inc(ready0, 1)
            dve.wait_ge(consts, 96)
            nc.vector.tensor_copy(sel[:, :, :].rearrange("p a n -> p (a n)"), sel_raw)
            nc.vector.tensor_copy(sel_last[:, :], sel_last_raw)
            dve.wait_ge(ready0, 2)
            nc.vector.tensor_tensor(r_lo[:, :], st_rT, r_hi[:, :].bitcast(f32), ALU.subtract).then_inc(ready0, 1)
            for b in range(BATCH):
                for half in range(2):
                    ln(2 * b + half, half)
            dve.wait_ge(ready0, 3)
            dve.wait_ge(lg_done, 1)
            rch = [0]

            def rlink(ins):
                rch[0] += 1
                ins.then_inc(wc_chain, 1)
                dve.wait_ge(wc_chain, rch[0])

            rlink(nc.vector.tensor_copy(lg[:, :, :].rearrange("p t e -> p (t e)"), mxp[:, 0, 0:16 * EXPERTS]))
            l_j = lg[:, :, :].unsqueeze(2).broadcast_to([128, 16, EXPERTS, EXPERTS])
            l_e = lg[:, :, :].unsqueeze(3).broadcast_to([128, 16, EXPERTS, EXPERTS])
            nc.vector.reduce_max(rt3[:, :], lg[:, :, :], AX)
            nc.vector.tensor_tensor(cmp_a, l_j, l_e, ALU.is_equal)
            rlink(nc.vector.tensor_tensor(cmp_b, l_j, l_e, ALU.is_gt))
            rlink(nc.vector.tensor_tensor(cmp_a, cmp_a, tie[:, :, :].unsqueeze(1).broadcast_to([128, 16, EXPERTS, EXPERTS]), ALU.mult))
            rlink(nc.vector.tensor_tensor(cmp_a, cmp_a, cmp_b, ALU.add))
            rlink(nc.vector.tensor_reduce(rt2[:, :, :], cmp_a, AX, ALU.add))
            rlink(nc.vector.tensor_scalar(rt2[:, :, :], rt2[:, :, :], 2.0, None, ALU.is_lt))
            nc.vector.tensor_tensor(rt1[:, :, :], lg[:, :, :], rt3[:, :].unsqueeze(2).broadcast_to([128, 16, EXPERTS]),
                                    ALU.subtract).then_inc(route_ln, 1)
            dve.wait_ge(route_ex, 1)
            rlink(nc.vector.tensor_tensor(rt2[:, :, :], rt2[:, :, :], rt1[:, :, :], ALU.mult))
            rlink(nc.vector.reduce_sum(rt3[:, :], rt2[:, :, :], AX))
            rlink(nc.vector.reciprocal(rt3[:, :], rt3[:, :]))
            nc.vector.tensor_tensor(lg[:, :, :], rt2[:, :, :], rt3[:, :].unsqueeze(2).broadcast_to([128, 16, EXPERTS]),
                                    ALU.mult).then_inc(route_g, 1)
            rlink(nc.vector.memset(gacc, 0.0))
            WC0 = rch[0]

            def c_weights(g, base, wk, u, wr, v):
                dve.wait_ge(cw_in, 64 * g + 64)
                for i, (w, uv, o) in enumerate(((wk, u, wku), (wr, v, wrv))):
                    nc.vector.tensor_tensor(w, w, uv, ALU.mult).then_inc(wc_chain, 1)
                    dve.wait_ge(wc_chain, base + i + 1)
                    last = nc.vector.tensor_reduce(o[:, :], w.rearrange("p (h d) -> p h d", d=DH), AX, ALU.add)
                last.then_inc(wc_done, 1)

            c_weights(0, WC0, *c_first)
            RC = WC0 + 2

            def gelu_lo(s, u, tc):
                for f in range(4):
                    dve.wait_ge(ghi_done, u * 4 + f + 1)
                    nc.vector.tensor_tensor(e_hid[tc % 2][1][:, f, :], e_h[tc % 2][:, f, :],
                                            e_hid[tc % 2][0][:, f, :].bitcast(f32), ALU.subtract).then_inc(glo_done, 1)

            def add_expert(s, u, tc):
                ts = slice(tc * HALF, (tc + 1) * HALF)
                dve.wait_ge(down_done, u + 3)
                dve.wait_ge(mo_acc, u + 8)
                nc.vector.scalar_tensor_tensor(e_tmp, acc_bank[tc % 2][:, :], bias_e[:, s, 4:5], gate_b[s][:, ts],
                                               op0=ALU.add, op1=ALU.mult).then_inc(wc_chain, 1)
                dve.wait_ge(wc_chain, u + RC + 1)
                nc.vector.tensor_tensor(gacc[:, ts], gacc[:, ts], e_tmp, ALU.add).then_inc(mo_acc, 1)

            def expert(s, ep, e, first=False):
                dve.wait_ge(e_in[s], ep * 48 + 48)
                for tc in range(4):
                    gelu_lo(s, e * 4 + tc, tc)
                    if tc > 0:
                        if tc == 1:
                            dve.wait_ge(gate_in[s], ep * 16 + 16)
                        add_expert(s, e * 4 + tc - 1, tc - 1)
                    elif not first:
                        add_expert(1 - s, e * 4 - 1, 3)

            for s in range(2):
                expert(s, 0, s, first=(s == 0))
            with dve.Fori(1, EXPERTS // 2) as ep:
                for s in range(2):
                    expert(s, ep, ep * 2 + s)
            add_expert(1, 4 * EXPERTS - 1, 3)
            dve.wait_ge(sig, 1)
            nc.vector.tensor_tensor(gacc, gacc, gate_b[0], ALU.mult).then_inc(gfin, 1)

            def reciprocals(g, part, rows):
                dve.wait_ge(rc_in, 32 * g + 16 * part + 16)
                nc.vector.reciprocal(rcp[rows, :], rc[rows, :]).then_inc(rc_chain, 1)
                dve.wait_ge(rc_chain, 4 * g + 2 * part + 1)
                nc.vector.tensor_copy(rc_hi[rows, :], rcp[rows, :]).then_inc(rc_chain, 1)
                dve.wait_ge(rc_chain, 4 * g + 2 * part + 2)
                nc.vector.tensor_tensor(rc_lo[rows, :], rcp[rows, :], rc_hi[rows, :].bitcast(f32), ALU.subtract).then_inc(rc_done, 1)

            def lo_half(m, i, src=pj):
                kq, c = i // 2, i % 2
                cs = slice(c * HALF, (c + 1) * HALF)
                dve.wait_ge(hi_done, 4 * m + i + 1)
                nc.vector.tensor_tensor(kq_lo[:, kq, cs], src[:, :], kq_hi[:, kq, cs].bitcast(f32), ALU.subtract)\
                    .then_inc(lo_done, 1)

            def max_reduce(m, t):
                half, h, j, c = t // 16, t // 8 % 2, t // 2 % 4, t % 2
                dve.wait_ge(mx_mm, 32 * m + t + 2)
                nc.vector.reduce_max(mx[:, half, h, j, c:c + 1], mxp[:, c, :], AX).then_inc(mx_red, 1)
                if t % 16 == 15:
                    dve.wait_ge(mx_red, 32 * m + t + 3)
                    nc.vector.tensor_tensor(mx_all[:, half, :, :], mx[:, half, :, :, 0], mx[:, half, :, :, 1],
                                            ALU.max).then_inc(m_chain, 1)
                    dve.wait_ge(m_chain, 4 * m + 2 * half + 1)
                    dve.wait_ge(m_row[half], 64 * m + 1)
                    nc.vector.tensor_scalar(m_hl[:, half, :, 0, :], mx_all[:, half, :, :], -1.0, None, ALU.mult).then_inc(m_chain, 1)
                    dve.wait_ge(m_chain, 4 * m + 2 * half + 2)
                    nc.vector.scalar_tensor_tensor(m_hl[:, half, :, 1, :], mx_all[:, half, :, :], -1.0,
                                                   m_hl[:, half, :, 0, :].bitcast(f32), op0=ALU.mult,
                                                   op1=ALU.subtract).then_inc(m_split, 1)

            def unit(g, p, prev=True, proj2=True, nxt=True):
                n = g * PAIRS + p
                queue = iter([(n + 1, t) for t in range(MX_TILES)] if prev else
                             [(n, t) for t in range(BEFORE, MX_TILES)] + [(n + 1, t) for t in range(MX_TILES)])
                for step in range(16):
                    half, kt = step // 8, step % 8
                    tiles = (MX_AT[step] if prev else FIRST_MX_AT[step]) if nxt else ""
                    for _ in range(len(tiles) - tiles.count("c")):
                        max_reduce(*next(queue))
                    pr, ac = probs[:, 2 * step % 4, :], acc[:, half, 0, :]
                    if step not in POOL_BOTH:
                        dve.wait_ge(exp_done, EXP0 + 32 * n + 2 * step + 5)
                    if kt == 0:
                        dve.wait_ge(sum_mm, 2 * n + half + 2)
                        nc.vector.tensor_copy(ac, pr).then_inc(add_done[0], 1)
                    elif step not in POOL_BOTH:
                        dve.wait_ge(add_done[0], 16 * n + step + 2)
                        nc.vector.tensor_tensor(ac, ac, pr, ALU.add).then_inc(add_done[0], 1)
                    if proj2 and step in PROJ_AT:
                        lo_half(n + 2, PROJ_AT[step])
                    if not nxt and step == RC_AT:
                        reciprocals(g, 0, slice(0, DONE))
                    for _ in range(tiles.count("c")):
                        max_reduce(*next(queue))

            with dve.Fori(0, BATCH) as b:
                with dve.Fori(0, LAYERS) as l:
                    g = b * LAYERS + l
                    n0 = g * PAIRS
                    for half in range(2):
                        hs = slice(half * HALF, (half + 1) * HALF)
                        dve.wait_ge(hh_done, 2 * g + half + 1)
                        nc.vector.tensor_tensor(h_lo[:, hs], hT[:, hs], h_hi[:, hs].bitcast(f32), ALU.subtract).then_inc(hl_done, 1)
                    for i in range(4):
                        lo_half(n0, i, first_bank[i])
                    for half in range(2):
                        dve.wait_ge(c_hi_done, 2 * g + half + 1)
                        hs = slice(half * HALF, (half + 1) * HALF)
                        nc.vector.tensor_tensor(c_hl[:, 1, hs], bank[half][0:HEADS, :], c_hl[:, 0, hs].bitcast(f32), ALU.subtract)\
                            .then_inc(c_lo_done, 1)
                    for t in range(16):
                        max_reduce(n0, t)
                    for i in range(4):
                        lo_half(n0 + 1, i, acc_bank[1 - i % 2])
                        for t in range(16 + 2 * i, 18 + 2 * i):
                            max_reduce(n0, t)
                    with dve.Fori(0, 1) as p:
                        unit(g, p, prev=False)
                    with dve.Fori(1, 6) as p:
                        unit(g, p)
                    with dve.Fori(6, 7) as p:
                        unit(g, p, proj2=False)
                    with dve.Fori(7, 8) as p:
                        unit(g, p, proj2=False, nxt=False)
                    for i in range(2 * PAIRS):
                        if i == 2 * PAIRS - 6:
                            dve.wait_ge(rrow_in, 32 * g + 32)
                            reciprocals(g, 1, slice(96, 128))
                        if i == 2 * PAIRS - 2:
                            dve.wait_ge(pv_ev, 2 * (n0 + PAIRS) + 1)
                        v = vecT[:, i // 2, (i % 2) * HALF:(i % 2 + 1) * HALF]
                        dve.wait_ge(bc_mm, 2 * PAIRS * g + i + 1)
                        nc.vector.tensor_tensor(v, bank[i % 4][:, :], v, ALU.mult).then_inc(vec_norm, 1)
                    for half in range(2):
                        hs = slice(half * HALF, (half + 1) * HALF)
                        dve.wait_ge(op_done, 2 * g + half + 2)
                        nc.vector.tensor_tensor(xT[:, hs], acc_bank[half][:, :], hT[:, hs], ALU.add).then_inc(x1_done, 1)
                    for k in range(2):
                        for half in range(2):
                            ln(4 * g + 4 + 2 * k + half, half)
                        if k == 0:
                            c_weights(g + 1, RC + 4 * EXPERTS + 2 * g, st_wk, st_u, st_wr, st_v)
                dve.wait_ge(ln_out, 4 * b * LAYERS + 4 * LAYERS + 4)
                dve.wait_ge(fin_in, b * 32 + 32)
                nc.vector.tensor_tensor(st_out, hT[:, :], st_wv, ALU.mult).then_inc(fin_done, 1)
                dve.wait_ge(fin_done, 2 * b + 3)
                nc.vector.tensor_tensor(st_out, st_out, st_x, ALU.add).then_inc(fin_done, 1)

        @block.gpsimd
        def _(pool):
            pool.wait_ge(seeded, 1)
            pool.wait_ge(ready0, 3)

            pool.wait_ge(ln_out, 4)
            for i in range(4):
                ts = slice(i * HALF, (i + 1) * HALF)
                last = nc.gpsimd.tensor_tensor(xn_hi[:, ts], xn[:, ts], zeros[:, :], ALU.add)
            last.then_inc(xn_chain, 1)
            pool.wait_ge(xn_chain, 1)
            nc.gpsimd.tensor_tensor(xn_lo, xn, xn_hi.bitcast(f32), ALU.subtract).then_inc(xn_split, 1)
            with pool.Fori(0, EXPERTS // 2) as ep:
                for s in range(2):
                    e = ep * 2 + s
                    raw_w = (e_up[s], e_dn[s].rearrange("p a n -> p (a n)"))
                    pool.wait_ge(e_in[s], ep * 48 + 48)
                    pool.wait_ge(mo_acc, e * 4 + 4)
                    for i in range(2):
                        nc.gpsimd.tensor_tensor(e_w[s][0][:, i * HALF:(i + 1) * HALF], raw_w[i], zeros[:, :],
                                                ALU.add).then_inc(ew_chain, 1)
                    for i in range(2):
                        pool.wait_ge(ew_chain, e * 2 + i + 1)
                        nc.gpsimd.tensor_tensor(e_w[s][1][:, i * HALF:(i + 1) * HALF], raw_w[i],
                                                e_w[s][0][:, i * HALF:(i + 1) * HALF].bitcast(f32),
                                                ALU.subtract).then_inc(ew_split, 1)

            def split_w(m):
                pool.wait_ge(wraw_in, 32 * m + 32)
                pool.wait_ge(proj, 4 * m + 1)
                nc.gpsimd.tensor_tensor(w_hi[:, :, :], w_raw[:, :, :], zeros[:, 0:384].rearrange("p (a n) -> p a n", a=3),
                                        ALU.add).then_inc(split_chain, 1)
                pool.wait_ge(split_chain, m + 1)
                nc.gpsimd.tensor_tensor(w_lo[:, :, :], w_raw[:, :, :], w_hi[:, :, :].bitcast(f32), ALU.subtract)\
                    .then_inc(w_split, 1)

            def unit(g, p, split2):
                n = g * PAIRS + p
                for step in range(16):
                    half, kt = step // 8, step % 8
                    if step in POOL_BOTH:
                        pool.wait_ge(exp_done, EXP0 + 32 * n + 2 * step + 5)
                        pool.wait_ge(add_done[0], 16 * n + step + 2)
                        nc.gpsimd.tensor_tensor(acc[:, half, 0, :], acc[:, half, 0, :], probs[:, 2 * step % 4, :],
                                                ALU.add).then_inc(add_done[0], 1)
                    pool.wait_ge(exp_done, EXP0 + 32 * n + 2 * step + 6)
                    pr, ac = probs[:, (2 * step + 1) % 4, :], acc[:, half, 1, :]
                    if kt == 0:
                        pool.wait_ge(sum_mm, 2 * n + half + 2)
                        nc.gpsimd.tensor_tensor(ac, pr, zeros[:, :], ALU.add).then_inc(add_done[1], 1)
                    else:
                        pool.wait_ge(add_done[1], 16 * n + step + 2)
                        nc.gpsimd.tensor_tensor(ac, ac, pr, ALU.add).then_inc(add_done[1], 1)
                    if split2 and step == SPLIT_AT:
                        split_w(n + 2)

            with pool.Fori(0, BATCH) as b:
                with pool.Fori(0, LAYERS) as l:
                    g = b * LAYERS + l
                    split_w(g * PAIRS)
                    pool.wait_ge(layer_in, 32 * g + 32)
                    for i in range(2):
                        cs = slice(i * HALF, (i + 1) * HALF)
                        last = nc.gpsimd.tensor_tensor(wv_hi[:, cs], st_wv[:, cs], zeros[:, :], ALU.add)
                    last.then_inc(wv_chain, 1)
                    pool.wait_ge(wv_chain, g + 1)
                    nc.gpsimd.tensor_tensor(wv_lo, st_wv, wv_hi.bitcast(f32), ALU.subtract).then_inc(wv_split, 1)
                    split_w(g * PAIRS + 1)
                    with pool.Fori(0, 3) as j:
                        unit(g, j * 2, True)
                        unit(g, j * 2 + 1, True)
                    with pool.Fori(6, 7) as p:
                        unit(g, p, False)
                    with pool.Fori(7, 8) as p:
                        unit(g, p, False)


def position_encoding(np):
    pos = np.arange(SEQ - 1, -1, -1, dtype=np.float32)
    freq = np.float32(1.0) / np.power(np.float32(10000.0), np.arange(0, D, 2, dtype=np.float32) / np.float32(D))
    ang = pos[:, None] * freq[None, :].astype(np.float32)
    return np.ascontiguousarray(np.concatenate([np.sin(ang), np.cos(ang)], axis=-1).T.astype(np.float32))


def kernel(**inputs):
    import numpy as np
    import concourse.bacc as bacc
    from concourse import mybir as _mybir
    from concourse.bass_utils import run_bass_kernel_spmd as run

    x = {k.replace("L0_attn_", "").replace("L0_", ""): np.asarray(v) for k, v in inputs.items()}
    c = np.ascontiguousarray
    sel = np.zeros((2 * HEADS, PAIRS, 128), np.float32)
    for r in range(2 * HEADS):
        h = r % HEADS
        sel[r, h // 2, 64 * (h % 2):64 * (h % 2) + 64] = 1.0
    sel_last = np.tile(np.repeat(np.eye(2, dtype=np.float32), 64, axis=1), (2, 1))
    tie = np.zeros((128, EXPERTS, EXPERTS), np.float32)
    for e in range(EXPERTS):
        tie[:, e, :e] = 1.0
    chunks = lambda b, n: b.reshape(b.shape[0], n, 128).transpose(0, 2, 1)
    par = [x[k].reshape(LAYERS, D, 1) for k in ("ln1_g", "ln1_b", "ln2_g", "ln2_b", "b_ff2")]
    arrays = {
        "xT": c(x["x"].reshape(TOK, D).T),
        "ident": np.eye(128, dtype=np.float32),
        "rT": position_encoding(np),
        "sel": sel.reshape(2 * HEADS, PAIRS * 128),
        "sel_last": sel_last,
        "tie": tie,
        "W_qkv": c(x["W_qkv"]), "W_r": c(x["W_r"]), "W_o": c(x["W_o"]),
        "W_k": c(np.concatenate([x["W_qkv"], x["W_qkv"][:1]])[:, :, HEADS * DH:2 * HEADS * DH]),
        "W_r_next": c(np.concatenate([x["W_r"], x["W_r"][:1]])),
        "W_ff1": c(x["W_ff1"]), "W_ff2": c(x["W_ff2"]),
        "u": c(x["u"].reshape(1, HEADS * DH)), "v": c(x["v"].reshape(1, HEADS * DH)),
        "par": c(np.concatenate(par + [chunks(x["b_ff1"], 4)], axis=2)),
        "w_routerT": c(x["ffn_w_router"].T),
        "w_upT": c(x["ffn_w_up"].transpose(0, 2, 1)),
        "w_downT": c(x["ffn_w_down"].transpose(0, 2, 1)),
        "bias_e": c(np.concatenate([chunks(x["ffn_b_up"], 4), x["ffn_b_down"].reshape(EXPERTS, D, 1)], axis=2)),
    }
    nc = bacc.Bacc("TRN2", target_bir_lowering=False, num_devices=1)
    args = {k: nc.dram_tensor("in_" + k, v.shape, _mybir.dt.from_np(v.dtype), kind="ExternalInput").ap()
            for k, v in arrays.items()}
    out = nc.dram_tensor("out_T", (D, TOK), _mybir.dt.float32, kind="ExternalOutput").ap()
    build(nc, args, out)
    r = run(nc, [{"in_" + k: v for k, v in arrays.items()}], core_ids=[0])
    return c(r.results[0]["out_T"].T).reshape(BATCH, SEQ, D)
```
